# Optimizing a Trainium2 kernel written in Bass

```python
import numpy as np
import jax
import jax.numpy as jnp

def _softmax(x, axis=-1):
    return jax.nn.softmax(x, axis=axis)

def _gelu(x):
    return jax.nn.gelu(x, approximate=True)

def _silu(x):
    return jax.nn.silu(x)

def _sigmoid(x):
    return jax.nn.sigmoid(x)

def _layernorm(x, axis=-1, eps=1e-05):
    m = jnp.mean(x, axis=axis, keepdims=True)
    v = jnp.var(x, axis=axis, keepdims=True)
    return (x - m) / jnp.sqrt(v + eps)

def _scatter_add(tgt, idx, src, axis=0):
    return tgt.at[idx].add(src)

def _segment_sum(src, seg, n):
    return jax.ops.segment_sum(src, seg, n)
kernel_name = 'mk_dlrm_tower_d1_rec_r8_06240c'

def setup_inputs(seed: int=0):
    np.random.seed(seed)
    _w = jnp.asarray

    def _rec_inputs():
        import jax
        import jax.numpy as jnp
        _tk = jax.random.key(seed)
        dense_ctx = jax.random.normal(jax.random.fold_in(_tk, 190), (512, 16), jnp.float32)
        ids = jnp.stack([jax.random.randint(jax.random.fold_in(_tk, 200 + f), (512,), 0, v, jnp.int32) for f, v in enumerate([1000, 12500, 1000, 125000, 1000, 125000, 1000, 12500, 12500, 1000, 1000, 1000, 125000, 125000, 1000, 1250, 125000, 12500, 1250, 125000, 1000, 1000, 1250, 125000, 12500, 1000, 12500, 12500, 1000, 1000, 1000, 1000, 1250, 1000, 1000, 1000, 1250, 1000, 1250, 1000, 1250, 1250, 1000, 1000, 1000, 1000, 1000, 1000])], axis=1)
        tbl_0 = 0.05 * jax.random.normal(jax.random.fold_in(_tk, 500 + 0), (1000, 32), jnp.float32)
        tbl_1 = 0.05 * jax.random.normal(jax.random.fold_in(_tk, 500 + 1), (12500, 32), jnp.float32)
        tbl_2 = 0.05 * jax.random.normal(jax.random.fold_in(_tk, 500 + 2), (1000, 32), jnp.float32)
        tbl_3 = 0.05 * jax.random.normal(jax.random.fold_in(_tk, 500 + 3), (125000, 32), jnp.float32)
        tbl_4 = 0.05 * jax.random.normal(jax.random.fold_in(_tk, 500 + 4), (1000, 32), jnp.float32)
        tbl_5 = 0.05 * jax.random.normal(jax.random.fold_in(_tk, 500 + 5), (125000, 32), jnp.float32)
        tbl_6 = 0.05 * jax.random.normal(jax.random.fold_in(_tk, 500 + 6), (1000, 32), jnp.float32)
        tbl_7 = 0.05 * jax.random.normal(jax.random.fold_in(_tk, 500 + 7), (12500, 32), jnp.float32)
        tbl_8 = 0.05 * jax.random.normal(jax.random.fold_in(_tk, 500 + 8), (12500, 32), jnp.float32)
        tbl_9 = 0.05 * jax.random.normal(jax.random.fold_in(_tk, 500 + 9), (1000, 32), jnp.float32)
        tbl_10 = 0.05 * jax.random.normal(jax.random.fold_in(_tk, 500 + 10), (1000, 32), jnp.float32)
        tbl_11 = 0.05 * jax.random.normal(jax.random.fold_in(_tk, 500 + 11), (1000, 32), jnp.float32)
        tbl_12 = 0.05 * jax.random.normal(jax.random.fold_in(_tk, 500 + 12), (125000, 32), jnp.float32)
        tbl_13 = 0.05 * jax.random.normal(jax.random.fold_in(_tk, 500 + 13), (125000, 32), jnp.float32)
        tbl_14 = 0.05 * jax.random.normal(jax.random.fold_in(_tk, 500 + 14), (1000, 32), jnp.float32)
        tbl_15 = 0.05 * jax.random.normal(jax.random.fold_in(_tk, 500 + 15), (1250, 32), jnp.float32)
        tbl_16 = 0.05 * jax.random.normal(jax.random.fold_in(_tk, 500 + 16), (125000, 32), jnp.float32)
        tbl_17 = 0.05 * jax.random.normal(jax.random.fold_in(_tk, 500 + 17), (12500, 32), jnp.float32)
        tbl_18 = 0.05 * jax.random.normal(jax.random.fold_in(_tk, 500 + 18), (1250, 32), jnp.float32)
        tbl_19 = 0.05 * jax.random.normal(jax.random.fold_in(_tk, 500 + 19), (125000, 32), jnp.float32)
        tbl_20 = 0.05 * jax.random.normal(jax.random.fold_in(_tk, 500 + 20), (1000, 32), jnp.float32)
        tbl_21 = 0.05 * jax.random.normal(jax.random.fold_in(_tk, 500 + 21), (1000, 32), jnp.float32)
        tbl_22 = 0.05 * jax.random.normal(jax.random.fold_in(_tk, 500 + 22), (1250, 32), jnp.float32)
        tbl_23 = 0.05 * jax.random.normal(jax.random.fold_in(_tk, 500 + 23), (125000, 32), jnp.float32)
        tbl_24 = 0.05 * jax.random.normal(jax.random.fold_in(_tk, 500 + 24), (12500, 32), jnp.float32)
        tbl_25 = 0.05 * jax.random.normal(jax.random.fold_in(_tk, 500 + 25), (1000, 32), jnp.float32)
        tbl_26 = 0.05 * jax.random.normal(jax.random.fold_in(_tk, 500 + 26), (12500, 32), jnp.float32)
        tbl_27 = 0.05 * jax.random.normal(jax.random.fold_in(_tk, 500 + 27), (12500, 32), jnp.float32)
        tbl_28 = 0.05 * jax.random.normal(jax.random.fold_in(_tk, 500 + 28), (1000, 32), jnp.float32)
        tbl_29 = 0.05 * jax.random.normal(jax.random.fold_in(_tk, 500 + 29), (1000, 32), jnp.float32)
        tbl_30 = 0.05 * jax.random.normal(jax.random.fold_in(_tk, 500 + 30), (1000, 32), jnp.float32)
        tbl_31 = 0.05 * jax.random.normal(jax.random.fold_in(_tk, 500 + 31), (1000, 32), jnp.float32)
        tbl_32 = 0.05 * jax.random.normal(jax.random.fold_in(_tk, 500 + 32), (1250, 32), jnp.float32)
        tbl_33 = 0.05 * jax.random.normal(jax.random.fold_in(_tk, 500 + 33), (1000, 32), jnp.float32)
        tbl_34 = 0.05 * jax.random.normal(jax.random.fold_in(_tk, 500 + 34), (1000, 32), jnp.float32)
        tbl_35 = 0.05 * jax.random.normal(jax.random.fold_in(_tk, 500 + 35), (1000, 32), jnp.float32)
        tbl_36 = 0.05 * jax.random.normal(jax.random.fold_in(_tk, 500 + 36), (1250, 32), jnp.float32)
        tbl_37 = 0.05 * jax.random.normal(jax.random.fold_in(_tk, 500 + 37), (1000, 32), jnp.float32)
        tbl_38 = 0.05 * jax.random.normal(jax.random.fold_in(_tk, 500 + 38), (1250, 32), jnp.float32)
        tbl_39 = 0.05 * jax.random.normal(jax.random.fold_in(_tk, 500 + 39), (1000, 32), jnp.float32)
        tbl_40 = 0.05 * jax.random.normal(jax.random.fold_in(_tk, 500 + 40), (1250, 32), jnp.float32)
        tbl_41 = 0.05 * jax.random.normal(jax.random.fold_in(_tk, 500 + 41), (1250, 32), jnp.float32)
        tbl_42 = 0.05 * jax.random.normal(jax.random.fold_in(_tk, 500 + 42), (1000, 32), jnp.float32)
        tbl_43 = 0.05 * jax.random.normal(jax.random.fold_in(_tk, 500 + 43), (1000, 32), jnp.float32)
        tbl_44 = 0.05 * jax.random.normal(jax.random.fold_in(_tk, 500 + 44), (1000, 32), jnp.float32)
        tbl_45 = 0.05 * jax.random.normal(jax.random.fold_in(_tk, 500 + 45), (1000, 32), jnp.float32)
        tbl_46 = 0.05 * jax.random.normal(jax.random.fold_in(_tk, 500 + 46), (1000, 32), jnp.float32)
        tbl_47 = 0.05 * jax.random.normal(jax.random.fold_in(_tk, 500 + 47), (1000, 32), jnp.float32)
        _rk = jax.random.fold_in(_tk, 7)
        W_top1 = 0.0472456 * jax.random.normal(jax.random.fold_in(_tk, 801), (448, 512), jnp.float32)
        W_top2 = 0.0441942 * jax.random.normal(jax.random.fold_in(_tk, 802), (512, 256), jnp.float32)
        W_top3 = 0.0625 * jax.random.normal(jax.random.fold_in(_tk, 803), (256, 1), jnp.float32)
        b_top1 = jnp.zeros((512,), jnp.float32)
        b_top2 = jnp.zeros((256,), jnp.float32)
        return (dense_ctx, ids, tbl_0, tbl_1, tbl_2, tbl_3, tbl_4, tbl_5, tbl_6, tbl_7, tbl_8, tbl_9, tbl_10, tbl_11, tbl_12, tbl_13, tbl_14, tbl_15, tbl_16, tbl_17, tbl_18, tbl_19, tbl_20, tbl_21, tbl_22, tbl_23, tbl_24, tbl_25, tbl_26, tbl_27, tbl_28, tbl_29, tbl_30, tbl_31, tbl_32, tbl_33, tbl_34, tbl_35, tbl_36, tbl_37, tbl_38, tbl_39, tbl_40, tbl_41, tbl_42, tbl_43, tbl_44, tbl_45, tbl_46, tbl_47, W_top1, b_top1, W_top2, b_top2, W_top3)
    dense_ctx, ids, tbl_0, tbl_1, tbl_2, tbl_3, tbl_4, tbl_5, tbl_6, tbl_7, tbl_8, tbl_9, tbl_10, tbl_11, tbl_12, tbl_13, tbl_14, tbl_15, tbl_16, tbl_17, tbl_18, tbl_19, tbl_20, tbl_21, tbl_22, tbl_23, tbl_24, tbl_25, tbl_26, tbl_27, tbl_28, tbl_29, tbl_30, tbl_31, tbl_32, tbl_33, tbl_34, tbl_35, tbl_36, tbl_37, tbl_38, tbl_39, tbl_40, tbl_41, tbl_42, tbl_43, tbl_44, tbl_45, tbl_46, tbl_47, W_top1, b_top1, W_top2, b_top2, W_top3 = _rec_inputs()

    def _L0_rec_setup():
        import jax, jax.numpy as jnp
        import numpy as np
        B, F, E = (1024, 48, 32)
        LAYER_SIZES = [128, 128, 128]

        def _cin_layer(xi, x0, W, b):
            Fi, F0 = (xi.shape[1], x0.shape[1])
            Wr = W.reshape(Fi, F0, -1)
            out = jnp.einsum('nie,nje,ijo->noe', xi, x0, Wr) + b[None, :, None]
            return jax.nn.relu(out)
        key = jax.random.key(seed)
        ks = jax.random.split(key, 1 + 2 * len(LAYER_SIZES))
        inputs = jax.random.normal(ks[0], (B, F, E), dtype=jnp.float32)
        out = {'inputs': inputs}
        prev = F
        for li, size in enumerate(LAYER_SIZES):
            in_ch = prev * F
            out[f'W{li + 1}'] = jax.random.normal(ks[1 + 2 * li], (in_ch, size), dtype=jnp.float32) * (1.0 / np.sqrt(in_ch))
            out[f'b{li + 1}'] = jnp.zeros((size,), dtype=jnp.float32)
            prev = size
        return out
    _L0_rec_all = _L0_rec_setup()
    _L0_rec_in = {k: v for k, v in _L0_rec_all.items() if k in ('W1', 'b1', 'W2', 'b2', 'W3', 'b3')}
    del _L0_rec_all
    return {'dense_ctx': dense_ctx, 'ids': ids, 'tbl_0': tbl_0, 'tbl_1': tbl_1, 'tbl_2': tbl_2, 'tbl_3': tbl_3, 'tbl_4': tbl_4, 'tbl_5': tbl_5, 'tbl_6': tbl_6, 'tbl_7': tbl_7, 'tbl_8': tbl_8, 'tbl_9': tbl_9, 'tbl_10': tbl_10, 'tbl_11': tbl_11, 'tbl_12': tbl_12, 'tbl_13': tbl_13, 'tbl_14': tbl_14, 'tbl_15': tbl_15, 'tbl_16': tbl_16, 'tbl_17': tbl_17, 'tbl_18': tbl_18, 'tbl_19': tbl_19, 'tbl_20': tbl_20, 'tbl_21': tbl_21, 'tbl_22': tbl_22, 'tbl_23': tbl_23, 'tbl_24': tbl_24, 'tbl_25': tbl_25, 'tbl_26': tbl_26, 'tbl_27': tbl_27, 'tbl_28': tbl_28, 'tbl_29': tbl_29, 'tbl_30': tbl_30, 'tbl_31': tbl_31, 'tbl_32': tbl_32, 'tbl_33': tbl_33, 'tbl_34': tbl_34, 'tbl_35': tbl_35, 'tbl_36': tbl_36, 'tbl_37': tbl_37, 'tbl_38': tbl_38, 'tbl_39': tbl_39, 'tbl_40': tbl_40, 'tbl_41': tbl_41, 'tbl_42': tbl_42, 'tbl_43': tbl_43, 'tbl_44': tbl_44, 'tbl_45': tbl_45, 'tbl_46': tbl_46, 'tbl_47': tbl_47, 'W_top1': W_top1, 'b_top1': b_top1, 'W_top2': W_top2, 'b_top2': b_top2, 'W_top3': W_top3, 'L0_rec_W1': _L0_rec_in['W1'], 'L0_rec_b1': _L0_rec_in['b1'], 'L0_rec_W2': _L0_rec_in['W2'], 'L0_rec_b2': _L0_rec_in['b2'], 'L0_rec_W3': _L0_rec_in['W3'], 'L0_rec_b3': _L0_rec_in['b3']}

def reference(dense_ctx, ids, tbl_0, tbl_1, tbl_2, tbl_3, tbl_4, tbl_5, tbl_6, tbl_7, tbl_8, tbl_9, tbl_10, tbl_11, tbl_12, tbl_13, tbl_14, tbl_15, tbl_16, tbl_17, tbl_18, tbl_19, tbl_20, tbl_21, tbl_22, tbl_23, tbl_24, tbl_25, tbl_26, tbl_27, tbl_28, tbl_29, tbl_30, tbl_31, tbl_32, tbl_33, tbl_34, tbl_35, tbl_36, tbl_37, tbl_38, tbl_39, tbl_40, tbl_41, tbl_42, tbl_43, tbl_44, tbl_45, tbl_46, tbl_47, W_top1, b_top1, W_top2, b_top2, W_top3, L0_rec_W1, L0_rec_b1, L0_rec_W2, L0_rec_b2, L0_rec_W3, L0_rec_b3):
    import jax
    import jax.numpy as jnp

    def _L0_rec_ref(inputs, W1, b1, W2, b2, W3, b3):
        import jax, jax.numpy as jnp
        import numpy as np
        B, F, E = (1024, 48, 32)
        LAYER_SIZES = [128, 128, 128]

        def _cin_layer(xi, x0, W, b):
            Fi, F0 = (xi.shape[1], x0.shape[1])
            Wr = W.reshape(Fi, F0, -1)
            out = jnp.einsum('nie,nje,ijo->noe', xi, x0, Wr) + b[None, :, None]
            return jax.nn.relu(out)
        x0 = inputs
        xs = [x0]
        for W, b in ((W1, b1), (W2, b2), (W3, b3)):
            xs.append(_cin_layer(xs[-1], x0, W, b))
        return jnp.concatenate(xs, axis=1).sum(axis=-1)
    e = jnp.stack([tbl_0[ids[:, 0]], tbl_1[ids[:, 1]], tbl_2[ids[:, 2]], tbl_3[ids[:, 3]], tbl_4[ids[:, 4]], tbl_5[ids[:, 5]], tbl_6[ids[:, 6]], tbl_7[ids[:, 7]], tbl_8[ids[:, 8]], tbl_9[ids[:, 9]], tbl_10[ids[:, 10]], tbl_11[ids[:, 11]], tbl_12[ids[:, 12]], tbl_13[ids[:, 13]], tbl_14[ids[:, 14]], tbl_15[ids[:, 15]], tbl_16[ids[:, 16]], tbl_17[ids[:, 17]], tbl_18[ids[:, 18]], tbl_19[ids[:, 19]], tbl_20[ids[:, 20]], tbl_21[ids[:, 21]], tbl_22[ids[:, 22]], tbl_23[ids[:, 23]], tbl_24[ids[:, 24]], tbl_25[ids[:, 25]], tbl_26[ids[:, 26]], tbl_27[ids[:, 27]], tbl_28[ids[:, 28]], tbl_29[ids[:, 29]], tbl_30[ids[:, 30]], tbl_31[ids[:, 31]], tbl_32[ids[:, 32]], tbl_33[ids[:, 33]], tbl_34[ids[:, 34]], tbl_35[ids[:, 35]], tbl_36[ids[:, 36]], tbl_37[ids[:, 37]], tbl_38[ids[:, 38]], tbl_39[ids[:, 39]], tbl_40[ids[:, 40]], tbl_41[ids[:, 41]], tbl_42[ids[:, 42]], tbl_43[ids[:, 43]], tbl_44[ids[:, 44]], tbl_45[ids[:, 45]], tbl_46[ids[:, 46]], tbl_47[ids[:, 47]]], axis=1)
    z = _L0_rec_ref(e, L0_rec_W1, L0_rec_b1, L0_rec_W2, L0_rec_b2, L0_rec_W3, L0_rec_b3)
    z = z.reshape(z.shape[0], -1)
    h = jnp.concatenate([z, dense_ctx], axis=1)
    h = jnp.maximum(h @ W_top1 + b_top1, 0.0)
    h = jnp.maximum(h @ W_top2 + b_top2, 0.0)
    y = h @ W_top3
    return y

_drawn_inputs = setup_inputs


def setup_inputs(seed=0):
    import zlib

    import numpy as np

    out = dict(_drawn_inputs(seed))
    spreads = {'b_top1': (0.0, 2.0),
     'b_top2': (0.0, 0.669),
     'L0_rec_b1': (0.0, 0.1),
     'L0_rec_b2': (0.0, 0.283),
     'L0_rec_b3': (0.0, 0.395)}
    factors = {'tbl_0': 8.0,
     'tbl_1': 3.391,
     'tbl_2': 8.0,
     'tbl_3': 7.949,
     'tbl_4': 8.0,
     'tbl_5': 8.0,
     'tbl_6': 7.232,
     'tbl_7': 4.923,
     'tbl_8': 4.999,
     'tbl_9': 8.0,
     'tbl_10': 8.0,
     'tbl_11': 8.0,
     'tbl_12': 6.769,
     'tbl_13': 8.0,
     'tbl_14': 8.0,
     'tbl_15': 6.204,
     'tbl_16': 8.0,
     'tbl_17': 8.0,
     'tbl_18': 8.0,
     'tbl_19': 5.64,
     'tbl_20': 8.0,
     'tbl_21': 5.728,
     'tbl_22': 8.0,
     'tbl_23': 8.0,
     'tbl_24': 8.0,
     'tbl_25': 8.0,
     'tbl_26': 6.971,
     'tbl_27': 8.0,
     'tbl_28': 8.0,
     'tbl_29': 8.0,
     'tbl_30': 8.0,
     'tbl_31': 8.0,
     'tbl_32': 8.0,
     'tbl_33': 2.814,
     'tbl_34': 6.981,
     'tbl_35': 8.0,
     'tbl_36': 8.0,
     'tbl_37': 8.0,
     'tbl_38': 8.0,
     'tbl_39': 7.795,
     'tbl_40': 8.0,
     'tbl_41': 4.506,
     'tbl_42': 6.833,
     'tbl_43': 6.637,
     'tbl_44': 5.544,
     'tbl_45': 8.0,
     'tbl_46': 8.0,
     'tbl_47': 4.429,
     'L0_rec_W1': 8.0,
     'L0_rec_W2': 8.0,
     'L0_rec_W3': 8.0,
     'dense_ctx': 7.495}
    for name, (base, spread) in spreads.items():
        noise = np.random.default_rng([zlib.crc32(name.encode()), seed]).standard_normal(out[name].shape)
        drawn = base * np.exp(spread * noise) if base else spread * noise
        out[name] = jnp.asarray(drawn.astype(out[name].dtype))
    for name, factor in factors.items():
        out[name] = (out[name] * factor).astype(out[name].dtype)
    return out
```

```python
from contextlib import ExitStack

import numpy as np

import concourse.bass as bass
import concourse.mybir as mybir

ROWS = [1000, 12500, 1000, 125000, 1000, 125000, 1000, 12500, 12500, 1000, 1000, 1000, 125000, 125000,
        1000, 1250, 125000, 12500, 1250, 125000, 1000, 1000, 1250, 125000, 12500, 1000, 12500, 12500,
        1000, 1000, 1000, 1000, 1250, 1000, 1000, 1000, 1250, 1000, 1250, 1000, 1250, 1250, 1000, 1000,
        1000, 1000, 1000, 1000]
F = len(ROWS)
E = 32
B = 512
P = 128
NB = B // P
TILES = NB * E
CTX = 16
SHIFTS = F // 2 + 1
PAIRS = F * (F + 1) // 2
KT = -(-PAIRS // P)
Z = KT * P
XW = F + SHIFTS - 1
Q = 4
BANKS = F // Q
RING = 6
HID1, HID2 = 512, 256

TAKES = "ADADAADADADA"
A_BANKS = [n for n in range(BANKS) if TAKES[n] == "A"]
D_BANKS = [n for n in range(BANKS) if TAKES[n] == "D"]
NA, ND = len(A_BANKS), len(D_BANKS)
PRODS, FMAS = Q * NA, Q * ND
SUMS = 7
FREED = {1: 1, 2: 1, 3: 2, 4: 2, 5: 4, 6: 6}
PAIR_BANK = (1, 0, 0)
EPI1, EPI2, EPI3 = 6, 9, 5

HALF_RANGE = 2.0 ** -13
TINY = 1e-30
EXPONENT = 0x7F800000


def build(nc, ids, tables, ctx_in, w_pair, w_pair_t, w2, w3, b_cin, wt1, bt1, wt2, bt2, wt3, out):
    f32, f16, i32, u32 = mybir.dt.float32, mybir.dt.float16, mybir.dt.int32, mybir.dt.uint32
    ALU, ACT, AX = mybir.AluOpType, mybir.ActivationFunctionType, mybir.AxisListType

    with ExitStack() as stack:
        def sb(name, shape, dt=f32):
            return stack.enter_context(nc.sbuf_tensor(name, shape, dt))

        def ps(name, shape, dt=f32):
            return stack.enter_context(nc.psum_tensor(name, shape, dt))

        def sem(name):
            return stack.enter_context(nc.semaphore(name))

        def wait(eng, s, value):
            if not (isinstance(value, int) and value <= 0):
                eng.wait_ge(s, value)

        ids_sb = sb("ids_sb", [P, NB, F], i32)
        emb = sb("emb", [P, NB, F, E])
        xx = sb("xx", [P, TILES, XW])
        work = sb("work", [P, NA * Q * P + 2 * Z])
        prods = work[:, 0:NA * Q * P].rearrange("p (a k o) -> p a (k o)", a=NA, k=Q)
        z = work[:, NA * Q * P:NA * Q * P + Z]
        zT = work[:, NA * Q * P + Z:NA * Q * P + 2 * Z].rearrange("p (t c) -> p t c", c=P)
        w1s = sb("w1s", [P, KT, P])
        w1b = sb("w1b", [P, KT, P])
        whi = [sb(f"whi{l}", [P, F * P], f16) for l in (2, 3)]
        wlo = [sb(f"wlo{l}", [P, F * P], f16) for l in (2, 3)]
        bcin = sb("bcin", [P, 3, P])
        brow = sb("brow", [1, 3 * P])
        ones = sb("ones", [1, P])
        eye32 = sb("eye32", [P, P])
        eye16 = sb("eye16", [P, P], f16)
        wmax = sb("wmax", [P, 16])
        wmaxr = sb("wmaxr", [1, 4])
        wpow = sb("wpow", [P, 2])
        xc = sb("xc", [P, 2, 2, F])
        hi = [sb(f"hi{l}", [P, P], f16) for l in (1, 2)]
        lo = [sb(f"lo{l}", [P, P], f16) for l in (1, 2)]
        xT = [sb(f"xT{l}", [P, 2, P], f16) for l in (1, 2)]
        acc = [sb(f"acc{l}", [P, Q * P]) for l in (2, 3)]
        part = sb("part", [P, 2, Q * P])
        half = [sb(f"half{l}", [P, 2 * P]) for l in (2, 3)]
        hs = [sb(f"hs{l}", [P, 2 * P]) for l in (2, 3)]
        ssum = [sb(f"ssum{l}", [P, P]) for l in (2, 3)]
        pre = [sb(f"pre{l}", [P, P]) for l in (1, 2, 3)]
        r = [sb(f"r{l}", [P, P]) for l in (1, 2, 3)]
        mx = [sb(f"mx{l}", [P, 2]) for l in (1, 2)]
        mp = [sb(f"mp{l}", [P, 2]) for l in (1, 2)]
        sc = [sb(f"sc{l}", [P, 1]) for l in (1, 2)]
        pooled = sb("pooled", [P, NB, 3, P])
        low = sb("low", [P, NB, F + CTX])
        hT = sb("hT", [P, 4, B])
        wt1_sb = sb("wt1_sb", [P, 4, HID1])
        wt2_sb = sb("wt2_sb", [P, HID1 // P, HID2])
        wt3_sb = sb("wt3_sb", [P, HID2 // P])
        bt1_sb = sb("bt1_sb", [P, HID1 // P])
        bt2_sb = sb("bt2_sb", [P, HID2 // P])
        y_sb = sb("y_sb", [1, B])
        h1 = xx[:, 0:29, :].rearrange("p t w -> p (t w)")[:, 0:4 * B].rearrange("p (c n) -> p c n", n=B)
        h2 = xx[:, 29:58, :].rearrange("p t w -> p (t w)")[:, 0:2 * B].rearrange("p (c n) -> p c n", n=B)
        raw = [xx[:, :, :].rearrange("p t w -> p (t w)")[:, 0:F * P], work[:, 0:F * P]]

        ybank = [ps(f"y{n}", [P, Q * P]) for n in range(RING)]
        misc = [ps(f"m{n}", [P, Q * P]) for n in range(2)]

        s_ids, s_in, s_top = sem("ids_loaded"), sem("small_loaded"), sem("top_loaded")
        s_w = [[sem(f"w{l}_{c}_loaded") for c in range(4)] for l in (2, 3)]
        s_gather = [sem(f"gathered{b}") for b in range(NB)]
        s_const = sem("constants_ready")
        s_wchain, s_wpe, s_split = sem("weight_scale_steps"), sem("weight_scale_pe"), sem("weights_hi")
        s_setup = sem("setup_done")
        s_xx = sem("xx_tiles")
        s_z, s_zt, s_zts = sem("z_ready"), sem("zT_in_psum"), sem("zT_saved")
        s_l1 = sem("layer1_in_psum")
        s_epi = [sem(f"epilogue{l}_steps") for l in (1, 2, 3)]
        s_hi = [sem(f"hi{l}_ready") for l in (1, 2)]
        s_xt, s_xts = [sem(f"xT{l}_in_psum") for l in (1, 2)], [sem(f"xT{l}_saved") for l in (1, 2)]
        s_y = [sem(f"y{l}_ready") for l in (2, 3)]
        s_prod = [sem(f"products{l}") for l in (2, 3)]
        s_fma = [sem(f"fmas{l}") for l in (2, 3)]
        s_sum = [sem(f"sums{l}") for l in (2, 3)]
        s_pool = [sem(f"pooled{l}") for l in (1, 2, 3)]
        s_xc = sem("xc_ready")
        s_tt, s_tts, s_low, s_h1p, s_h1, s_h2p, s_h2, s_yp, s_ys, s_out = (
            sem(n) for n in ("hT_in_psum", "hT_saved", "low_ready", "h1_in_psum", "h1_ready", "h2_in_psum",
                             "h2_ready", "y_in_psum", "y_ready", "y_stored"))

        def bank_done(eng, layer, tile, n):
            if TAKES[n] == "A":
                wait(eng, s_prod[layer], tile * PRODS + Q * (A_BANKS.index(n) + 1))
            else:
                wait(eng, s_fma[layer], tile * FMAS + Q * (D_BANKS.index(n) + 1))

        def steps(eng, step):
            for v in (-3, -2, -1, 0):
                step(v, v % 2)
            with eng.Fori(0, (TILES - 4) // 2) as pair:
                step(pair * 2 + 1, 1)
                step(pair * 2 + 2, 0)
            for v in (TILES - 3, TILES - 2, TILES - 1):
                step(v, v % 2)

        def active(tile):
            return not isinstance(tile, int) or 0 <= tile < TILES

        block = stack.enter_context(nc.Block())

        @block.sync
        def _(sp):
            sp.dma_start(ids_sb[:], ids.rearrange("(b p) f -> p b f", p=P)).then_inc(s_ids, 16)
            for l, w in enumerate((w2, w3)):
                for c in range(4):
                    n = F * P // 4
                    sp.dma_start(raw[l][:, c * n:(c + 1) * n], w[:, c * n:(c + 1) * n]).then_inc(s_w[l][c], 16)
            sp.dma_start(w1s[:], w_pair).then_inc(s_in, 16)
            sp.dma_start(w1b[:], w_pair_t).then_inc(s_in, 16)
            for l in range(3):
                sp.dma_start(brow[:, l * P:(l + 1) * P], b_cin[l].rearrange("(a n) -> a n", a=1)).then_inc(s_in, 16)
            sp.dma_start(low[:, :, F:F + CTX], ctx_in.rearrange("(b p) c -> p b c", p=P)).then_inc(s_top, 16)
            sp.dma_start(wt1_sb[0:F, 0, :], wt1[0:F, :]).then_inc(s_top, 16)
            sp.dma_start(wt1_sb[F:F + CTX, 0, :], wt1[F + 3 * P:F + 3 * P + CTX, :]).then_inc(s_top, 16)
            sp.dma_start(wt1_sb[:, 1:4, :], wt1[F:F + 3 * P, :].rearrange("(c p) n -> p c n", p=P)).then_inc(s_top, 16)
            sp.dma_start(wt2_sb[:], wt2.rearrange("(c p) n -> p c n", p=P)).then_inc(s_top, 16)
            with nc.allow_non_contiguous_dma(reason="a few hundred bias and weight scalars"):
                sp.dma_start(wt3_sb[:], wt3.rearrange("(c p) n -> p (c n)", p=P)).then_inc(s_top, 16)
                sp.dma_start(bt1_sb[:], bt1.rearrange("(c p) -> p c", p=P)).then_inc(s_top, 16)
                sp.dma_start(bt2_sb[:], bt2.rearrange("(c p) -> p c", p=P)).then_inc(s_top, 16)
            sp.wait_ge(s_ys, 1)
            sp.dma_start(out.rearrange("n a -> a n"), y_sb[:]).then_inc(s_out, 16)
            sp.wait_ge(s_out, 16)

        @block.gpsimd
        def _(pool):
            def gather(b, fields):
                for f in fields:
                    pool.indirect_dma_start(
                        emb[:, b, f, :], None, tables[f],
                        bass.IndirectOffsetOnAxis(ap=ids_sb[:, b, f:f + 1], axis=0)).then_inc(s_gather[b], 16)

            def spread(b, e0, n):
                t0 = b * E + e0
                src = emb[:, b, :, e0:e0 + n].rearrange("p f e -> p e f")
                pool.wait_ge(s_gather[b], 16 * F)
                pool.tensor_copy(xx[:, t0:t0 + n, 0:F], src).then_inc(s_xx, n // 2)
                pool.tensor_copy(xx[:, t0:t0 + n, F:XW], src[:, :, 0:XW - F]).then_inc(s_xx, n // 2)

            pool.wait_ge(s_ids, 16)
            gather(0, range(2))
            pool.memset(eye32[:], 0.0).then_inc(s_const, 1)
            pool.memset(eye16[:], 0.0).then_inc(s_const, 1)
            pool.memset(ones[:], 1.0).then_inc(s_const, 1)
            for l in range(3):
                pool.memset(pooled[:, :, l, :], 0.0).then_inc(s_pool[l], 1)
            pool.wait_ge(s_const, 3)
            for m in (eye32, eye16):
                pool.affine_select(out=m[:], in_=m[:], compare_op=ALU.not_equal, fill=1.0, base=0,
                                   pattern=[[-1, P]], channel_multiplier=1).then_inc(s_const, 1)
            gather(0, range(2, F))

            def sums(layer, tile, first):
                s, done = s_sum[layer], tile * SUMS
                a, b = part[:, 0, :], part[:, 1, :]

                def add(o, x, y):
                    pool.tensor_tensor(o, x, y, ALU.add).then_inc(s, 1)

                for w in first:
                    wait(pool, *w)
                wait(pool, s_prod[layer], tile * PRODS + 3 * Q)
                add(a, prods[:, 1, :], prods[:, 2, :])
                wait(pool, s_prod[layer], tile * PRODS + 5 * Q)
                add(b, prods[:, 3, :], prods[:, 4, :])
                wait(pool, s, done + 2)
                add(a, a, b)
                wait(pool, s_prod[layer], tile * PRODS + 6 * Q)
                wait(pool, s, done + 3)
                add(a, a, prods[:, 5, :])
                wait(pool, s, done + 4)
                wait(pool, s_epi[layer + 1], (tile - 1) * (EPI2, EPI3)[layer] + 2)
                add(half[layer][:], a[:, 0:2 * P], a[:, 2 * P:4 * P])
                wait(pool, s_prod[layer], tile * PRODS + 7 * Q)
                add(b[:, 0:2 * P], prods[:, 6, 0:2 * P], prods[:, 6, 2 * P:4 * P])
                wait(pool, s, done + 6)
                add(half[layer][:], half[layer][:], b[:, 0:2 * P])

            def over_e(l, tile, block_of, value):
                if not active(tile):
                    return
                wait(pool, s_epi[l], value)
                wait(pool, s_pool[l], tile + 1)
                dst = pooled[:, block_of, l, :]
                pool.tensor_tensor(dst, dst, r[l][:], ALU.add).then_inc(s_pool[l], 1)

            def step(v, b1, b2, b3):
                over_e(1, v, b2, v * EPI2 + 5)
                if active(v + 1):
                    sums(0, v + 1, [(s_sum[1], v * SUMS)] if active(v) else [])
                over_e(2, v - 1, b3, (v - 1) * EPI3 + 5)
                if active(v):
                    sums(1, v, [(s_sum[0], (v + 2) * SUMS)] if active(v + 1) else [])
                over_e(0, v + 2, b1, (v + 2) * EPI1 + 2)

            def run(v0, v1, b1, b2, b3):
                if isinstance(v0, int) and (v1 - v0 == 1 or v0 < 1):
                    for v in range(v0, v1):
                        step(v, b1, b2, b3)
                elif v1 > v0:
                    with pool.Fori(v0, v1) as v:
                        step(v, b1, b2, b3)

            for v in (-3, -2, -1):
                step(v, 0, 0, 0)
            step(0, 0, 0, 0)
            for b in range(NB):
                v0, end = b * E + 1, (b + 1) * E - 2
                if b + 1 < NB:
                    for g in range(8):
                        gather(b + 1, range(6 * g, 6 * g + 6))
                        run(v0, v0 + 3, b, b, b)
                        v0 += 3
                    for g in range(4):
                        spread(b + 1, 8 * g, 8)
                        run(v0, v0 + 1, b, b, b)
                        v0 += 1
                    run(v0, end, b, b, b)
                    step(end, b + 1, b, b)
                    step(end + 1, b + 1, b, b)
                    step(end + 2, b + 1, b + 1, b)
                else:
                    run(v0, end, b, b, b)
                    step(end, None, b, b)
                    step(end + 1, None, b, b)
            over_e(2, TILES - 1, NB - 1, TILES * EPI3)

        @block.tensor
        def _(pe):
            pe.wait_ge(s_const, 5)
            pe.wait_ge(s_wchain, 9)
            nc.tensor.transpose(misc[0][0:1, 0:P], wmax[:, 8:9], eye32[:]).then_inc(s_wpe, 1)
            pe.wait_ge(s_wchain, 12)
            nc.tensor.matmul(misc[0][:, 0:1], ones[:], wmaxr[:, 2:3], start=True, stop=True).then_inc(s_wpe, 1)
            pe.wait_ge(s_in, 5 * 16)
            nc.tensor.matmul(misc[1][:, 0:3 * P], ones[:], brow[:], start=True, stop=True).then_inc(s_wpe, 1)
            pe.wait_ge(s_setup, 5)

            def transpose_pairs(t, g):
                if g == 0:
                    wait(pe, s_z, t + 1)
                elif g == 1:
                    wait(pe, s_epi[0], (t - 1) * EPI1 + 1)
                if g == 0 and active(t - 3):
                    wait(pe, s_xts[1], t - 2)
                elif g == 0:
                    wait(pe, s_xts[0], t - 1)
                elif g == 2:
                    wait(pe, s_zts, t * 3 + 2)
                ks = range(4 * g, min(4 * g + 4, KT))
                for k in ks:
                    ins = nc.tensor.transpose(misc[PAIR_BANK[g]][:, (k % 4) * P:(k % 4 + 1) * P],
                                              z[:, k * P:(k + 1) * P], eye32[:])
                ins.then_inc(s_zt, 1)

            def layer1(t, c):
                if c == 0:
                    wait(pe, s_zts, t * 3 + 3)
                for k in (2 * c, 2 * c + 1):
                    ins = nc.tensor.matmul(misc[0][:, 0:P], zT[:, k, :], w1s[:, k, :],
                                           start=k == 0, stop=k == KT - 1)
                if 2 * c + 2 == KT:
                    ins.then_inc(s_l1, 1)

            def transpose_x(l, t):
                wait(pe, s_hi[l], t + 1)
                wait(pe, s_epi[l], (t + 1) * (EPI1, EPI2)[l])
                dst = misc[1][:, 0:P].bitcast(f16)
                nc.tensor.transpose(dst[:, 0:P], hi[l][:], eye16[:])
                nc.tensor.transpose(dst[:, P:2 * P], lo[l][:], eye16[:]).then_inc(s_xt[l], 1)

            def y_item(layer, t, n):
                if n == 0:
                    wait(pe, s_xts[layer], t + 1)
                dst = ybank[n % RING]
                cols = slice(n * Q * P, (n + 1) * Q * P)
                for m, (a, w) in enumerate(((0, whi), (0, wlo), (1, whi))):
                    ins = nc.tensor.matmul(dst[:], xT[layer][:, a, :], w[layer][:, cols], start=m == 0, stop=m == 2)
                ins.then_inc(s_y[layer], 1)

            def step(v, parity):
                t0, t1, t2, t3 = v + 3, v + 2, v + 1, v
                for n in range(2 * BANKS):
                    if n in (11, 14, 20) and active(t0):
                        transpose_pairs(t0, (11, 14, 20).index(n))
                    if 2 <= n < 7 and active(t1):
                        layer1(t1, n - 2)
                    if n == 4 and active(t3):
                        if active(t2):
                            wait(pe, s_xts[0], t2 + 1)
                        else:
                            wait(pe, s_xts[1], t3)
                        transpose_x(1, t3)
                    if n == 18 and active(t1):
                        if active(t0):
                            wait(pe, s_zts, t0 * 3 + 1)
                        else:
                            wait(pe, s_xts[1], t3 + 1)
                        transpose_x(0, t1)
                    m = n % BANKS
                    if n < BANKS and active(t2):
                        if m >= RING:
                            bank_done(pe, 0, t2, m - RING)
                        elif active(t3 - 1):
                            bank_done(pe, 1, t3 - 1, m + RING)
                        else:
                            bank_done(pe, 0, t2 - 1, m + RING)
                        y_item(0, t2, m)
                    if n >= BANKS and active(t3):
                        if m >= RING:
                            bank_done(pe, 1, t3, m - RING)
                        elif active(t2):
                            bank_done(pe, 0, t2, m + RING)
                        else:
                            bank_done(pe, 1, t3 - 1, m + RING)
                        y_item(1, t3, m)

            steps(pe, step)

            for l in range(3):
                pe.wait_ge(s_pool[l], TILES + 1)
            bank_done(pe, 1, TILES - 1, BANKS - 1)
            bank_done(pe, 1, TILES - 1, BANKS - 2)
            for c in (1, 2, 3):
                for b in range(NB):
                    ins = nc.tensor.transpose(ybank[c][:, b * P:(b + 1) * P], pooled[:, b, c - 1, :], eye32[:])
                ins.then_inc(s_tt, 1)
            pe.wait_ge(s_low, 1)
            pe.wait_ge(s_top, 8 * 16)
            for b in range(NB):
                ins = nc.tensor.transpose(ybank[0][0:F + CTX, b * P:(b + 1) * P], low[:, b, :], eye32[:])
            ins.then_inc(s_tt, 1)
            h1bank = [ybank[4], ybank[5], misc[0], misc[1]]
            wait(pe, s_epi[0], TILES * EPI1)
            wait(pe, s_xts[1], TILES)
            for step_, c in enumerate((1, 2, 3, 0)):
                pe.wait_ge(s_tts, step_ + 1)
                k = F + CTX if c == 0 else P
                for m in range(HID1 // P):
                    ins = nc.tensor.matmul(h1bank[m][:], wt1_sb[0:k, c, m * P:(m + 1) * P], hT[0:k, c, :],
                                           start=c == 1, stop=c == 0)
                    if c == 0:
                        ins.then_inc(s_h1p, 1)
            for c in range(HID1 // P):
                pe.wait_ge(s_h1, c + 1)
                for m in range(HID2 // P):
                    ins = nc.tensor.matmul(ybank[1 + m][:], wt2_sb[:, c, m * P:(m + 1) * P], h1[:, c, :],
                                           start=c == 0, stop=c == HID1 // P - 1)
            ins.then_inc(s_h2p, 1)
            for c in range(HID2 // P):
                pe.wait_ge(s_h2, c + 1)
                ins = nc.tensor.matmul(ybank[3][0:1, :], wt3_sb[:, c:c + 1], h2[:, c, :],
                                       start=c == 0, stop=c == HID2 // P - 1)
            ins.then_inc(s_yp, 1)

        @block.scalar
        def _(act):
            act.wait_ge(s_wchain, 14)
            for l in range(2):
                nc.scalar.activation(whi[l][:], raw[l], ACT.Copy, scale=wpow[:, 1:2]).then_inc(s_split, 1)

            act.wait_ge(s_setup, 5)

            def products(layer, t, n, free):
                a = A_BANKS.index(n)
                wait(act, s_y[layer], t * BANKS + n + 1)
                for w in free:
                    wait(act, *w)
                col = xc[:, parity_now[0], 1 - layer, :]
                for k in range(Q):
                    j = n * Q + k
                    nc.scalar.activation(prods[:, a, k * P:(k + 1) * P], ybank[n % RING][:, k * P:(k + 1) * P],
                                         ACT.Copy, scale=col[:, j:j + 1]).then_inc(s_prod[layer], 1)

            def free_of(layer, t, a):
                if a == 0:
                    return s_fma[layer], t * FMAS + Q
                return s_sum[layer], t * SUMS + FREED[a]

            def save_pairs(t, g):
                wait(act, s_zt, t * 3 + g + 1)
                if g == 0:
                    wait(act, s_l1, t)
                n = min(4, KT - 4 * g)
                nc.scalar.activation(zT[:, 4 * g:4 * g + n, :].rearrange("p t c -> p (t c)"),
                                     misc[PAIR_BANK[g]][:, 0:n * P], ACT.Copy).then_inc(s_zts, 1)

            def hi_part(l, t):
                wait(act, s_epi[l], t * (EPI1, EPI2)[l] + (5, 8)[l])
                wait(act, s_xt[l], t)
                nc.scalar.activation(hi[l][:], r[l][:], ACT.Copy, scale=sc[l][:]).then_inc(s_hi[l], 1)

            def save_x(l, t):
                wait(act, s_xt[l], t + 1)
                wait(act, s_y[l], t * BANKS)
                nc.scalar.activation(xT[l][:].rearrange("p a c -> p (a c)"), misc[1][:, 0:P].bitcast(f16),
                                     ACT.Copy).then_inc(s_xts[l], 1)

            parity_now = [0]

            def step(v, parity):
                t1, t2, t3 = v + 2, v + 1, v
                parity_now[0] = parity
                wait(act, s_xc, v + 2)
                for n in range(2 * BANKS):
                    if n < BANKS and active(t2) and TAKES[n] == "A":
                        a = A_BANKS.index(n)
                        products(0, t2, n, [free_of(1, t3 - 1, a) if active(t3 - 1) else free_of(0, t2 - 1, a)])
                    if n >= BANKS and active(t3) and TAKES[n - BANKS] == "A":
                        a = A_BANKS.index(n - BANKS)
                        products(1, t3, n - BANKS, [free_of(0, t2, a) if active(t2) else free_of(1, t3 - 1, a)])
                    if n == 5 and active(t3):
                        save_x(1, t3)
                    if n == 9 and active(t1):
                        hi_part(0, t1)
                    if n in (11, 14, 21) and active(t1 + 1):
                        save_pairs(t1 + 1, (11, 14, 21).index(n))
                    if n == 19 and active(t1):
                        save_x(0, t1)
                    if n == 22 and active(t2):
                        hi_part(1, t2)

            steps(act, step)

            for i, c in enumerate((1, 2, 3, 0)):
                k = F + CTX if c == 0 else P
                act.wait_ge(s_tt, i + 1)
                nc.scalar.activation(hT[0:k, c, :], ybank[c][0:k, :], ACT.Copy).then_inc(s_tts, 1)
            act.wait_ge(s_top, 8 * 16)
            h1bank = [ybank[4], ybank[5], misc[0], misc[1]]
            for m in range(HID1 // P):
                act.wait_ge(s_h1p, m + 1)
                nc.scalar.activation(h1[:, m, :], h1bank[m][:], ACT.Relu, bias=bt1_sb[:, m:m + 1]).then_inc(s_h1, 1)
            act.wait_ge(s_h2p, 1)
            for m in range(HID2 // P):
                nc.scalar.activation(h2[:, m, :], ybank[1 + m][:], ACT.Relu, bias=bt2_sb[:, m:m + 1]).then_inc(s_h2, 1)
            act.wait_ge(s_yp, 1)
            nc.scalar.activation(y_sb[:], ybank[3][0:1, :], ACT.Copy).then_inc(s_ys, 1)

        @block.vector
        def _(dve):
            for l in range(2):
                for c in range(4):
                    dve.wait_ge(s_w[l][c], 16)
                    n = F * P // 4
                    nc.vector.tensor_reduce(wmax[:, 4 * l + c:4 * l + c + 1], raw[l][:, c * n:(c + 1) * n], axis=AX.X,
                                            op=ALU.max, apply_absolute_value=True).then_inc(s_wchain, 1)
            dve.wait_ge(s_wchain, 8)
            nc.vector.tensor_reduce(wmax[:, 8:9], wmax[:, 0:8], axis=AX.X, op=ALU.max).then_inc(s_wchain, 1)
            dve.wait_ge(s_wpe, 1)
            nc.vector.tensor_reduce(wmaxr[:, 0:1], misc[0][0:1, 0:P], axis=AX.X, op=ALU.max).then_inc(s_wchain, 1)
            dve.wait_ge(s_wchain, 10)
            nc.vector.tensor_scalar(wmaxr[:, 1:2], wmaxr[:, 0:1], TINY, HALF_RANGE, ALU.max, ALU.mult).then_inc(s_wchain, 1)
            dve.wait_ge(s_wchain, 11)
            nc.vector.tensor_scalar(wmaxr[:, 2:3].bitcast(u32), wmaxr[:, 1:2].bitcast(u32), EXPONENT, None,
                                    ALU.bitwise_and).then_inc(s_wchain, 1)
            dve.wait_ge(s_wpe, 2)
            nc.vector.tensor_copy(wpow[:, 0:1], misc[0][:, 0:1]).then_inc(s_wchain, 1)
            dve.wait_ge(s_wchain, 13)
            nc.vector.reciprocal(wpow[:, 1:2], wpow[:, 0:1]).then_inc(s_wchain, 1)
            dve.wait_ge(s_wpe, 3)
            nc.vector.tensor_copy(bcin[:].rearrange("p l o -> p (l o)"), misc[1][:, 0:3 * P]).then_inc(s_setup, 1)
            dve.wait_ge(s_in, 5 * 16)
            nc.vector.tensor_tensor(w1s[:], w1s[:], w1b[:], ALU.add).then_inc(s_setup, 1)
            dve.wait_ge(s_wchain, 14)
            for l in range(2):
                dve.wait_ge(s_split, l + 1)
                nc.vector.scalar_tensor_tensor(wlo[l][:], raw[l], wpow[:, 1:2], whi[l][:], ALU.mult,
                                               ALU.subtract).then_inc(s_setup, 1)
            dve.wait_ge(s_setup, 4)
            nc.vector.memset(z[:, SHIFTS * F:Z], 0.0).then_inc(s_setup, 1)
            src = emb[:, 0].rearrange("p f e -> p e f")
            dve.wait_ge(s_gather[0], 16 * F)
            nc.vector.tensor_copy(xx[:, 0:E, 0:F], src).then_inc(s_xx, E // 2)
            nc.vector.tensor_copy(xx[:, 0:E, F:XW], src[:, :, 0:XW - F]).then_inc(s_xx, E // 2)
            dve.wait_ge(s_xx, E)

            def pair_products(t):
                wait(dve, s_xx, t + 1)
                wait(dve, s_zt, t * 3)
                row = xx[:, bass.ds(t, 1), :].rearrange("p a w -> p (a w)")
                base = row[:, 0:F]
                rep = bass.AP(base.tensor, base.offset, [base.ap[0], [0, SHIFTS], [1, F]])
                win = bass.AP(base.tensor, base.offset, [base.ap[0], [1, SHIFTS], [1, F]])
                nc.vector.tensor_tensor(z[:, 0:SHIFTS * F].rearrange("p (d i) -> p d i", i=F), rep, win,
                                        ALU.mult).then_inc(s_z, 1)

            def columns(v, parity):
                t3, t2 = v + 1, v + 2
                if not active(t3) and not active(t2):
                    return
                wait(dve, s_xx, (t2 if active(t2) else t3) + 1)
                wait(dve, s_prod[1], v * PRODS)
                wait(dve, s_prod[0], (v + 1) * PRODS)
                k0, k1 = (0 if active(t3) else 1), (2 if active(t2) else 1)
                nc.vector.tensor_scalar(xc[:, 1 - parity, k0:k1, :], xx[:, bass.ds(t3 + k0, k1 - k0), 0:F],
                                        wpow[:, 0:1], None, ALU.mult).then_inc(s_xc, 1)

            def fma(layer, t, q, parity):
                n, k = D_BANKS[q // Q], q % Q
                j = n * Q + k
                if k == 0:
                    wait(dve, s_y[layer], t * BANKS + n + 1)
                dst = acc[layer][:, k * P:(k + 1) * P]
                if q < Q:
                    wait(dve, s_prod[layer], t * PRODS + k + 1)
                    if k == 0:
                        wait(dve, s_epi[layer + 1], (t - 1) * (EPI2, EPI3)[layer] + 1)
                    add = prods[:, 0, k * P:(k + 1) * P]
                else:
                    wait(dve, s_fma[layer], t * FMAS + q - Q + 1)
                    add = dst
                nc.vector.scalar_tensor_tensor(dst, ybank[n % RING][:, k * P:(k + 1) * P],
                                               xc[:, parity, 1 - layer, j:j + 1], add, ALU.mult,
                                               ALU.add).then_inc(s_fma[layer], 1)

            def scale_steps(l, t, parity, s, done):
                def clamp():
                    wait(dve, s, done)
                    nc.vector.tensor_scalar(mx[l][:, 1:2], mx[l][:, 0:1], TINY, HALF_RANGE, ALU.max,
                                            ALU.mult).then_inc(s, 1)

                def mask():
                    wait(dve, s, done + 1)
                    nc.vector.tensor_scalar(mp[l][:, parity:parity + 1].bitcast(u32), mx[l][:, 1:2].bitcast(u32),
                                            EXPONENT, None, ALU.bitwise_and).then_inc(s, 1)

                def invert():
                    wait(dve, s, done + 2)
                    wait(dve, s_hi[l], t)
                    nc.vector.reciprocal(sc[l][:], mp[l][:, parity:parity + 1]).then_inc(s, 1)

                return [clamp, mask, invert]

            def relu_max(l, t, s, done):
                wait(dve, s, done)
                wait(dve, s_pool[l], t + 1)
                wait(dve, s_hi[l], t)
                nc.vector.tensor_scalar(r[l][:], pre[l][:], 0.0, None, ALU.max, ALU.max,
                                        accum_out=mx[l][:, 0:1]).then_inc(s, 1)

            def lo_part(l, t):
                n = (EPI1, EPI2)[l]
                wait(dve, s_hi[l], t + 1)
                wait(dve, s_xt[l], t)
                wait(dve, s_epi[l], t * n + n - 1)
                nc.vector.scalar_tensor_tensor(lo[l][:], r[l][:], sc[l][:], hi[l][:], ALU.mult,
                                               ALU.subtract).then_inc(s_epi[l], 1)

            def epilogue1(t, parity):
                s, done = s_epi[0], t * EPI1

                def bias():
                    wait(dve, s_l1, t + 1)
                    nc.vector.tensor_tensor(pre[0][:], misc[0][:, 0:P], bcin[:, 0, :], ALU.add).then_inc(s, 1)

                return [bias, lambda: relu_max(0, t, s, done + 1), *scale_steps(0, t, parity, s, done + 2)]

            def merge(layer, t, parity, s, done):
                def own():
                    wait(dve, s_fma[layer], (t + 1) * FMAS)
                    nc.vector.tensor_tensor(hs[layer][:], acc[layer][:, 0:2 * P], acc[layer][:, 2 * P:4 * P],
                                            ALU.add).then_inc(s, 1)

                def pools():
                    wait(dve, s_sum[layer], (t + 1) * SUMS)
                    wait(dve, s, done + 1)
                    nc.vector.tensor_tensor(hs[layer][:], hs[layer][:], half[layer][:], ALU.add).then_inc(s, 1)

                def last():
                    wait(dve, s, done + 2)
                    nc.vector.tensor_tensor(ssum[layer][:], hs[layer][:, 0:P], hs[layer][:, P:2 * P],
                                            ALU.add).then_inc(s, 1)

                def bias():
                    wait(dve, s, done + 3)
                    nc.vector.scalar_tensor_tensor(pre[layer + 1][:], ssum[layer][:], mp[layer][:, parity:parity + 1],
                                                   bcin[:, layer + 1, :], ALU.mult, ALU.add).then_inc(s, 1)

                return [own, pools, last, bias]

            def epilogue2(t, parity):
                s, done = s_epi[1], t * EPI2
                return [*merge(0, t, parity, s, done), lambda: relu_max(1, t, s, done + 4),
                        *scale_steps(1, t, parity, s, done + 5)]

            def epilogue3(t, parity):
                s, done = s_epi[2], t * EPI3

                def relu():
                    wait(dve, s, done + 4)
                    wait(dve, s_pool[2], t + 1)
                    nc.vector.tensor_scalar(r[2][:], pre[2][:], 0.0, None, ALU.max).then_inc(s, 1)

                return [*merge(1, t, parity, s, done), relu]

            def step(v, parity):
                t1, t2, t3 = v + 2, v + 1, v
                other = 1 - parity
                wait(dve, s_xc, v + 2)
                todo = []

                def bank(layer, t, n):
                    d = D_BANKS.index(n)
                    for k in range(Q):
                        if active(t):
                            fma(layer, t, d * Q + k, parity)
                        if todo:
                            todo.pop(0)()

                def flush():
                    while todo:
                        todo.pop(0)()

                for n in range(2 * BANKS):
                    if TAKES[n % BANKS] != "D":
                        continue
                    if n == 6 and active(t1):
                        todo += epilogue1(t1, parity)
                    if n == 8 and active(t3 - 1):
                        todo += epilogue3(t3 - 1, other)
                    if n == 18 and active(t2):
                        todo += epilogue2(t2, other)
                    bank(n // BANKS, (t2, t3)[n // BANKS], n % BANKS)
                    if n == 3 and active(t1 + 1):
                        pair_products(t1 + 1)
                    if n == 10:
                        flush()
                        if active(t1):
                            lo_part(0, t1)
                    if n == 13:
                        columns(v, parity)
                flush()
                if active(t2):
                    lo_part(1, t2)

            steps(dve, step)
            for chained in epilogue3(TILES - 1, 1):
                chained()
            nc.vector.tensor_reduce(low[:, :, 0:F], emb[:], axis=AX.X, op=ALU.add).then_inc(s_low, 1)


def pair_rows():
    pairs = [(i, (i + d) % F) for d in range(SHIFTS) for i in range(F)][:PAIRS]
    first = np.array([i * F + j for i, j in pairs])
    second = np.array([j * F + i for i, j in pairs])
    return first, second


def kernel(**inputs):
    import concourse.bacc as bacc
    from concourse.bass_utils import run_bass_kernel_spmd

    nc = bacc.Bacc("TRN2", target_bir_lowering=False, num_devices=1)
    arrays = {}

    def given(name, a):
        a = np.ascontiguousarray(a)
        arrays[name] = a
        return nc.dram_tensor(name, a.shape, mybir.dt.from_np(a.dtype), kind="ExternalInput").ap()

    first, second = pair_rows()
    w1 = np.asarray(inputs["L0_rec_W1"])

    def by_tile(rows, off_diagonal):
        w = np.zeros((Z, P), w1.dtype)
        w[off_diagonal:PAIRS] = w1[rows[off_diagonal:]]
        return w.reshape(KT, P, P).transpose(1, 0, 2)

    ids = given("ids", inputs["ids"])
    tables = [given(f"tbl_{f}", inputs[f"tbl_{f}"]) for f in range(F)]
    args = [
        given("dense_ctx", inputs["dense_ctx"]),
        given("w_pair", by_tile(first, 0)),
        given("w_pair_t", by_tile(second, F)),
        given("w2", np.asarray(inputs["L0_rec_W2"]).reshape(P, F * P)),
        given("w3", np.asarray(inputs["L0_rec_W3"]).reshape(P, F * P)),
        [given(f"b{l}", inputs[f"L0_rec_b{l}"]) for l in (1, 2, 3)],
        given("W_top1", inputs["W_top1"]), given("b_top1", inputs["b_top1"]),
        given("W_top2", inputs["W_top2"]), given("b_top2", inputs["b_top2"]),
        given("W_top3", inputs["W_top3"]),
    ]
    out = nc.dram_tensor("out", (B, 1), mybir.dt.float32, kind="ExternalOutput").ap()
    build(nc, ids, tables, *args, out)
    result = run_bass_kernel_spmd(nc, [arrays], core_ids=[0])
    return result.results[0]["out"]
```

```python
from contextlib import ExitStack

import numpy as np

import concourse.bass as bass
import concourse.mybir as mybir

ROWS = [1000, 12500, 1000, 125000, 1000, 125000, 1000, 12500, 12500, 1000, 1000, 1000, 125000, 125000,
        1000, 1250, 125000, 12500, 1250, 125000, 1000, 1000, 1250, 125000, 12500, 1000, 12500, 12500,
        1000, 1000, 1000, 1000, 1250, 1000, 1000, 1000, 1250, 1000, 1250, 1000, 1250, 1250, 1000, 1000,
        1000, 1000, 1000, 1000]
F = len(ROWS)
E = 32
B = 512
P = 128
NB = B // P
TILES = NB * E
CTX = 16
SHIFTS = F // 2 + 1
PAIRS = F * (F + 1) // 2
KT = -(-PAIRS // P)
Z = KT * P
Q = 4
BANKS = F // Q
RING = 6
HID1, HID2 = 512, 256

TAKES = ("ADADAADADADA", "ADADADADADAD")
A_BANKS = [[n for n in range(BANKS) if t[n] == "A"] for t in TAKES]
D_BANKS = [[n for n in range(BANKS) if t[n] == "D"] for t in TAKES]
NA = [len(a) for a in A_BANKS]
PRODS, FMAS = [Q * len(a) for a in A_BANKS], [Q * len(d) for d in D_BANKS]
SUMS = (7, 6)
FREED = ({1: 1, 2: 1, 3: 2, 4: 2, 5: 4, 6: 6}, {1: 1, 2: 1, 3: 2, 4: 2, 5: 5})
CHUNKS = (1, 2, 0, 3)
TBANK = {1: 0, 2: 1, 0: 2, 3: 5}
GATHERS, SPREADS = 3, 4
PAIR_BANK = (1, 0, 0)
EPI0 = 6
EPI1, EPI2, EPI3 = 6, 9, 5

HALF_RANGE = 2.0 ** -13
TINY0 = 1e-15
TINY = 1e-30
EXPONENT = 0x7F800000


def build(nc, ids, tables, ctx_in, select, pairs_of, w_pair, w_pair_t, w2, w3, b_cin, wt1, bt1, wt2, bt2, wt3, out):
    f32, f16, i32, u32 = mybir.dt.float32, mybir.dt.float16, mybir.dt.int32, mybir.dt.uint32
    ALU, ACT, AX = mybir.AluOpType, mybir.ActivationFunctionType, mybir.AxisListType

    with ExitStack() as stack:
        def sb(name, shape, dt=f32):
            return stack.enter_context(nc.sbuf_tensor(name, shape, dt))

        def ps(name, shape, dt=f32):
            return stack.enter_context(nc.psum_tensor(name, shape, dt))

        def sem(name):
            return stack.enter_context(nc.semaphore(name))

        def wait(eng, s, value):
            if not (isinstance(value, int) and value <= 0):
                eng.wait_ge(s, value)

        ids_sb = sb("ids_sb", [P, NB, F], i32)
        emb = sb("emb", [P, NB, F, E])
        xx = sb("xx", [P, TILES, F])
        work = sb("work", [P, F * P])
        prods = work[:, 0:max(NA) * Q * P].rearrange("p (a k o) -> p a (k o)", a=max(NA), k=Q)
        zT = work[:, max(NA) * Q * P:max(NA) * Q * P + Z].rearrange("p (t c) -> p t c", c=P)
        w1s = sb("w1s", [P, KT, P])
        w1b = sb("w1b", [P, KT, P])
        wsq = sb("wsq", [P, KT, P])
        sel = sb("sel", [2 * F, Z], f16)
        member = sb("member", [P, KT, F])
        x0hl = sb("x0hl", [P, 2 * F], f16)
        x0T = sb("x0T", [2 * F, P], f16)
        mx0, sc0 = sb("mx0", [P, 2]), sb("sc0", [P, 1])
        mp0, msq = sb("mp0", [P, 1]), sb("msq", [P, 2])
        whi = [sb(f"whi{l}", [P, F * P], f16) for l in (2, 3)]
        wlo = [sb(f"wlo{l}", [P, F * P], f16) for l in (2, 3)]
        bcin = sb("bcin", [P, 3, P])
        brow = sb("brow", [1, 3 * P])
        ones = sb("ones", [1, P])
        eye32 = sb("eye32", [P, P])
        eye16 = sb("eye16", [P, P], f16)
        wmax = sb("wmax", [P, 16])
        wmaxr = sb("wmaxr", [1, 4])
        wpow = sb("wpow", [P, 2])
        xc = sb("xc", [P, 2, 2, F])
        hi = [sb(f"hi{l}", [P, P], f16) for l in (1, 2)]
        lo = [sb(f"lo{l}", [P, P], f16) for l in (1, 2)]
        xT = [sb(f"xT{l}", [P, 2, P], f16) for l in (1, 2)]
        acc = [sb(f"acc{l}", [P, Q * P]) for l in (2, 3)]
        part = sb("part", [P, 2, Q * P])
        half = [sb(f"half{l}", [P, 2 * P]) for l in (2, 3)]
        hs = [sb(f"hs{l}", [P, 2 * P]) for l in (2, 3)]
        ssum = [sb(f"ssum{l}", [P, P]) for l in (2, 3)]
        pre = [sb(f"pre{l}", [P, P]) for l in (1, 2, 3)]
        r = [sb(f"r{l}", [P, P]) for l in (1, 2, 3)]
        mx = [sb(f"mx{l}", [P, 2]) for l in (1, 2)]
        mp = [sb(f"mp{l}", [P, 2]) for l in (1, 2)]
        sc = [sb(f"sc{l}", [P, 1]) for l in (1, 2)]
        pooled = sb("pooled", [P, NB, 3, P])
        low = sb("low", [P, NB, F + CTX])
        hT = sb("hT", [P, 4, B])
        wt1_sb = sb("wt1_sb", [P, 4, HID1])
        wt2_sb = sb("wt2_sb", [P, HID1 // P, HID2])
        wt3_sb = sb("wt3_sb", [P, HID2 // P])
        bt1_sb = sb("bt1_sb", [P, HID1 // P])
        bt2_sb = sb("bt2_sb", [P, HID2 // P])
        y_sb = sb("y_sb", [1, B])
        flat = xx[:].rearrange("p t w -> p (t w)")
        h1 = flat[:, 0:4 * B].rearrange("p (c n) -> p c n", n=B)
        h2 = flat[:, 4 * B:6 * B].rearrange("p (c n) -> p c n", n=B)
        raw = [flat, work[:]]

        ybank = [ps(f"y{n}", [P, Q * P]) for n in range(RING)]
        misc = [ps(f"m{n}", [P, Q * P]) for n in range(2)]

        s_ids, s_in, s_top = sem("ids_loaded"), sem("small_loaded"), sem("top_loaded")
        s_w = [[sem(f"w{l}_{c}_loaded") for c in range(4)] for l in (2, 3)]
        s_gather = [sem(f"gathered{b}") for b in range(NB)]
        s_const = sem("constants_ready")
        s_wchain, s_wpe, s_split = sem("weight_scale_steps"), sem("weight_scale_pe"), sem("weights_hi")
        s_setup = sem("setup_done")
        s_xx = sem("xx_tiles")
        s_epi0, s_x0hi = sem("x0_steps"), sem("x0_hi")
        s_x0t, s_x0ts = sem("x0T_in_psum"), sem("x0T_saved")
        s_zt, s_zts = sem("pair_sums_in_psum"), sem("squares_saved")
        s_l1 = sem("layer1_in_psum")
        s_epi = [sem(f"epilogue{l}_steps") for l in (1, 2, 3)]
        s_hi = [sem(f"hi{l}_ready") for l in (1, 2)]
        s_xt, s_xts = [sem(f"xT{l}_in_psum") for l in (1, 2)], [sem(f"xT{l}_saved") for l in (1, 2)]
        s_y = [sem(f"y{l}_ready") for l in (2, 3)]
        s_prod = [sem(f"products{l}") for l in (2, 3)]
        s_fma = [sem(f"fmas{l}") for l in (2, 3)]
        s_sum = [sem(f"sums{l}") for l in (2, 3)]
        s_pool = [sem(f"pooled{l}") for l in (1, 2, 3)]
        s_xc = sem("xc_ready")
        s_tt, s_tts, s_low, s_h1p, s_h1, s_h2p, s_h2, s_yp, s_ys, s_out = (
            sem(n) for n in ("hT_in_psum", "hT_saved", "low_ready", "h1_in_psum", "h1_ready", "h2_in_psum",
                             "h2_ready", "y_in_psum", "y_ready", "y_stored"))

        def bank_done(eng, layer, tile, n):
            if n in A_BANKS[layer]:
                wait(eng, s_prod[layer], tile * PRODS[layer] + Q * (A_BANKS[layer].index(n) + 1))
            else:
                wait(eng, s_fma[layer], tile * FMAS[layer] + Q * (D_BANKS[layer].index(n) + 1))

        def steps(eng, step):
            for v in range(-4, 1):
                step(v, v % 2)
            with eng.Fori(0, (TILES - 6) // 2) as pair:
                step(pair * 2 + 1, 1)
                step(pair * 2 + 2, 0)
            for v in range(TILES - 5, TILES):
                step(v, v % 2)

        def active(tile):
            return not isinstance(tile, int) or 0 <= tile < TILES

        block = stack.enter_context(nc.Block())

        @block.sync
        def _(sp):
            sp.dma_start(ids_sb[:], ids.rearrange("(b p) f -> p b f", p=P)).then_inc(s_ids, 16)
            for l, w in enumerate((w2, w3)):
                for c in range(4):
                    n = F * P // 4
                    sp.dma_start(raw[l][:, c * n:(c + 1) * n], w[:, c * n:(c + 1) * n]).then_inc(s_w[l][c], 16)
            sp.dma_start(w1s[:], w_pair).then_inc(s_in, 16)
            sp.dma_start(w1b[:], w_pair_t).then_inc(s_in, 16)
            sp.dma_start(sel[:], select).then_inc(s_in, 16)
            sp.dma_start(member[:], pairs_of).then_inc(s_in, 16)
            for l in range(3):
                sp.dma_start(brow[:, l * P:(l + 1) * P], b_cin[l].rearrange("(a n) -> a n", a=1)).then_inc(s_in, 16)
            sp.dma_start(low[:, :, F:F + CTX], ctx_in.rearrange("(b p) c -> p b c", p=P)).then_inc(s_top, 16)
            sp.dma_start(wt1_sb[0:F, 0, :], wt1[0:F, :]).then_inc(s_top, 16)
            sp.dma_start(wt1_sb[F:F + CTX, 0, :], wt1[F + 3 * P:F + 3 * P + CTX, :]).then_inc(s_top, 16)
            sp.dma_start(wt1_sb[:, 1:4, :], wt1[F:F + 3 * P, :].rearrange("(c p) n -> p c n", p=P)).then_inc(s_top, 16)
            sp.dma_start(wt2_sb[:], wt2.rearrange("(c p) n -> p c n", p=P)).then_inc(s_top, 16)
            with nc.allow_non_contiguous_dma(reason="a few hundred bias and weight scalars"):
                sp.dma_start(wt3_sb[:], wt3.rearrange("(c p) n -> p (c n)", p=P)).then_inc(s_top, 16)
                sp.dma_start(bt1_sb[:], bt1.rearrange("(c p) -> p c", p=P)).then_inc(s_top, 16)
                sp.dma_start(bt2_sb[:], bt2.rearrange("(c p) -> p c", p=P)).then_inc(s_top, 16)
            sp.wait_ge(s_ys, 1)
            sp.dma_start(out.rearrange("n a -> a n"), y_sb[:]).then_inc(s_out, 16)
            sp.wait_ge(s_out, 16)

        @block.gpsimd
        def _(pool):
            def gather(b, fields):
                for f in fields:
                    pool.indirect_dma_start(
                        emb[:, b, f, :], None, tables[f],
                        bass.IndirectOffsetOnAxis(ap=ids_sb[:, b, f:f + 1], axis=0)).then_inc(s_gather[b], 16)

            def spread(b, e0, n):
                t0 = b * E + e0
                src = emb[:, b, :, e0:e0 + n].rearrange("p f e -> p e f")
                pool.wait_ge(s_gather[b], 16 * F)
                pool.tensor_copy(xx[:, t0:t0 + n, :], src).then_inc(s_xx, n)

            pool.wait_ge(s_ids, 16)
            gather(0, range(2))
            pool.memset(eye32[:], 0.0).then_inc(s_const, 1)
            pool.memset(eye16[:], 0.0).then_inc(s_const, 1)
            pool.memset(ones[:], 1.0).then_inc(s_const, 1)
            for l in range(3):
                pool.memset(pooled[:, :, l, :], 0.0).then_inc(s_pool[l], 1)
            pool.wait_ge(s_const, 3)
            for m in (eye32, eye16):
                pool.affine_select(out=m[:], in_=m[:], compare_op=ALU.not_equal, fill=1.0, base=0,
                                   pattern=[[-1, P]], channel_multiplier=1).then_inc(s_const, 1)
            gather(0, range(2, F))

            def sums(layer, tile, first):
                s, done = s_sum[layer], tile * SUMS[layer]
                a, b = part[:, 0, :], part[:, 1, :]

                def add(o, x, y):
                    pool.tensor_tensor(o, x, y, ALU.add).then_inc(s, 1)

                def written(m):
                    wait(pool, s_prod[layer], tile * PRODS[layer] + (m + 1) * Q)

                for w in first:
                    wait(pool, *w)
                written(2)
                add(a, prods[:, 1, :], prods[:, 2, :])
                written(4)
                add(b, prods[:, 3, :], prods[:, 4, :])
                wait(pool, s, done + 2)
                add(a, a, b)
                n = 3
                if NA[layer] == 7:
                    written(5)
                    wait(pool, s, done + 3)
                    add(a, a, prods[:, 5, :])
                    n = 4
                wait(pool, s, done + n)
                wait(pool, s_epi[layer + 1], (tile - 1) * (EPI2, EPI3)[layer] + 2)
                add(half[layer][:], a[:, 0:2 * P], a[:, 2 * P:4 * P])
                last = NA[layer] - 1
                written(last)
                add(b[:, 0:2 * P], prods[:, last, 0:2 * P], prods[:, last, 2 * P:4 * P])
                wait(pool, s, done + n + 2)
                add(half[layer][:], half[layer][:], b[:, 0:2 * P])

            def over_e(l, tile, block_of, value):
                if not active(tile):
                    return
                wait(pool, s_epi[l], value)
                wait(pool, s_pool[l], tile + 1)
                dst = pooled[:, block_of, l, :]
                pool.tensor_tensor(dst, dst, r[l][:], ALU.add).then_inc(s_pool[l], 1)

            def step(v, b1, b2, b3, between=lambda i: None):
                over_e(1, v, b2, v * EPI2 + 5)
                between(0)
                if active(v + 1):
                    sums(0, v + 1, [(s_sum[1], v * SUMS[1])] if active(v) else [])
                between(1)
                over_e(2, v - 1, b3, (v - 1) * EPI3 + 5)
                if active(v):
                    sums(1, v, [(s_sum[0], (v + 2) * SUMS[0])] if active(v + 1) else [])
                between(2)
                over_e(0, v + 2, b1, (v + 2) * EPI1 + 2)

            def run(v0, v1, b):
                with pool.Fori(v0, v1) as v:
                    step(v, b, b, b)

            for v in range(-4, 1):
                step(v, 0, 0, 0)
            for b in range(NB):
                v0, end = b * E + 1, (b + 1) * E - 2
                if b + 1 < NB:
                    for g in range(F // GATHERS):
                        step(v0, b, b, b, lambda i: gather(b + 1, range(GATHERS * g, GATHERS * (g + 1))[i:i + 1]))
                        v0 += 1
                    for g in range(SPREADS):
                        n = E // SPREADS
                        step(v0, b, b, b, lambda i: spread(b + 1, n * g, n) if i == 1 else None)
                        v0 += 1
                run(v0, end, b)
                step(end, b + 1, b, b)
                step(end + 1, b + 1, b, b)
                if b + 1 < NB:
                    step(end + 2, b + 1, b + 1, b)
            over_e(2, TILES - 1, NB - 1, TILES * EPI3)

        @block.tensor
        def _(pe):
            pe.wait_ge(s_const, 5)
            pe.wait_ge(s_wchain, 9)
            nc.tensor.transpose(misc[0][0:1, 0:P], wmax[:, 8:9], eye32[:]).then_inc(s_wpe, 1)
            pe.wait_ge(s_wchain, 12)
            nc.tensor.matmul(misc[0][:, 0:1], ones[:], wmaxr[:, 2:3], start=True, stop=True).then_inc(s_wpe, 1)
            pe.wait_ge(s_in, 7 * 16)
            nc.tensor.matmul(misc[1][:, 0:3 * P], ones[:], brow[:], start=True, stop=True).then_inc(s_wpe, 1)
            pe.wait_ge(s_setup, 2)
            for k in range(KT):
                ins = nc.tensor.matmul(misc[0][0:F, P:2 * P], member[:, k, :], w1s[:, k, :], start=k == 0, stop=k == KT - 1)
            ins.then_inc(s_wpe, 1)
            pe.wait_ge(s_setup, 6)

            def transpose_x0(t):
                wait(pe, s_epi0, (t + 1) * EPI0)
                wait(pe, s_x0hi, t + 1)
                wait(pe, s_xts[0], t - 1)
                nc.tensor.transpose(misc[1][0:2 * F, 0:P // 2].bitcast(f16), x0hl[:], eye16[:]).then_inc(s_x0t, 1)

            def pair_sums(t, g):
                if g == 0:
                    wait(pe, s_x0ts, t + 1)
                    wait(pe, s_xts[1], t - 2)
                elif g == 1:
                    wait(pe, s_epi[0], (t - 1) * EPI1 + 1)
                else:
                    wait(pe, s_zts, t * 3 + 2)
                for k in range(4 * g, min(4 * g + 4, KT)):
                    ins = nc.tensor.matmul(misc[PAIR_BANK[g]][:, (k % 4) * P:(k % 4 + 1) * P],
                                           sel[:, k * P:(k + 1) * P], x0T[:], start=True, stop=True)
                ins.then_inc(s_zt, 1)

            def layer1(t, c):
                if c == 0:
                    wait(pe, s_zts, t * 3 + 3)
                for k in (2 * c, 2 * c + 1):
                    ins = nc.tensor.matmul(misc[0][:, 0:P], zT[:, k, :], wsq[:, k, :],
                                           start=k == 0, stop=k == KT - 1)
                if 2 * c + 2 == KT:
                    ins.then_inc(s_l1, 1)

            def transpose_x(l, t):
                wait(pe, s_hi[l], t + 1)
                wait(pe, s_epi[l], (t + 1) * (EPI1, EPI2)[l])
                dst = misc[1][:, 0:P].bitcast(f16)
                nc.tensor.transpose(dst[:, 0:P], hi[l][:], eye16[:])
                nc.tensor.transpose(dst[:, P:2 * P], lo[l][:], eye16[:]).then_inc(s_xt[l], 1)

            def y_item(layer, t, n):
                if n == 0:
                    wait(pe, s_xts[layer], t + 1)
                dst = ybank[n % RING]
                cols = slice(n * Q * P, (n + 1) * Q * P)
                for m, (a, w) in enumerate(((0, whi), (0, wlo), (1, whi))):
                    ins = nc.tensor.matmul(dst[:], xT[layer][:, a, :], w[layer][:, cols], start=m == 0, stop=m == 2)
                ins.then_inc(s_y[layer], 1)

            def step(v, parity):
                t0, t1, t2, t3 = v + 3, v + 2, v + 1, v
                for n in range(2 * BANKS):
                    if n == 0 and active(t0):
                        transpose_x0(t0)
                    if n in (12, 14, 20) and active(t0):
                        pair_sums(t0, (12, 14, 20).index(n))
                    if 2 <= n < 7 and active(t1):
                        layer1(t1, n - 2)
                    if n == 6 and active(t3):
                        if active(t0):
                            wait(pe, s_x0ts, t0 + 1)
                        elif active(t2):
                            wait(pe, s_xts[0], t2 + 1)
                        else:
                            wait(pe, s_xts[1], t3)
                        transpose_x(1, t3)
                    if n == 18 and active(t1):
                        if active(t0):
                            wait(pe, s_zts, t0 * 3 + 1)
                        else:
                            wait(pe, s_xts[1], t3 + 1)
                        transpose_x(0, t1)
                    m = n % BANKS
                    if n < BANKS and active(t2):
                        if m >= RING:
                            bank_done(pe, 0, t2, m - RING)
                        elif active(t3 - 1):
                            bank_done(pe, 1, t3 - 1, m + RING)
                        else:
                            bank_done(pe, 0, t2 - 1, m + RING)
                        y_item(0, t2, m)
                    if n >= BANKS and active(t3):
                        if m >= RING:
                            bank_done(pe, 1, t3, m - RING)
                        elif active(t2):
                            bank_done(pe, 0, t2, m + RING)
                        else:
                            bank_done(pe, 1, t3 - 1, m + RING)
                        y_item(1, t3, m)

            steps(pe, step)

            last = TILES - 1
            pe.wait_ge(s_top, 8 * 16)
            for l in (0, 1):
                pe.wait_ge(s_pool[l], TILES + 1)
                bank_done(pe, 1, last, RING + TBANK[l + 1])
                for b in range(NB):
                    ins = nc.tensor.transpose(ybank[TBANK[l + 1]][:, b * P:(b + 1) * P], pooled[:, b, l, :], eye32[:])
                ins.then_inc(s_tt, 1)
            pe.wait_ge(s_low, NB)
            bank_done(pe, 1, last, RING + TBANK[0])
            for b in range(NB):
                ins = nc.tensor.transpose(ybank[TBANK[0]][0:F + CTX, b * P:(b + 1) * P], low[:, b, :], eye32[:])
            ins.then_inc(s_tt, 1)
            wait(pe, s_epi[0], TILES * EPI1)
            wait(pe, s_xts[1], TILES)
            h1bank = [misc[0], misc[1], ybank[3], ybank[4]]
            bank_done(pe, 1, last, RING + 3)
            bank_done(pe, 1, last, RING + 4)
            for i, c in enumerate(CHUNKS):
                if c == 3:
                    pe.wait_ge(s_pool[2], TILES + 1)
                    bank_done(pe, 1, last, RING + TBANK[3])
                    for b in range(NB):
                        ins = nc.tensor.transpose(ybank[TBANK[3]][:, b * P:(b + 1) * P], pooled[:, b, 2, :], eye32[:])
                    ins.then_inc(s_tt, 1)
                pe.wait_ge(s_tts, i + 1)
                k = F + CTX if c == 0 else P
                for m in range(HID1 // P):
                    ins = nc.tensor.matmul(h1bank[m][:], wt1_sb[0:k, c, m * P:(m + 1) * P], hT[0:k, c, :],
                                           start=i == 0, stop=c == 3)
                    if c == 3:
                        ins.then_inc(s_h1p, 1)
            for c in range(HID1 // P):
                pe.wait_ge(s_h1, c + 1)
                for m in range(HID2 // P):
                    ins = nc.tensor.matmul(ybank[m][:], wt2_sb[:, c, m * P:(m + 1) * P], h1[:, c, :],
                                           start=c == 0, stop=c == HID1 // P - 1)
                    if c == HID1 // P - 1:
                        ins.then_inc(s_h2p, 1)
            for c in range(HID2 // P):
                pe.wait_ge(s_h2, c + 1)
                ins = nc.tensor.matmul(ybank[2][0:1, :], wt3_sb[:, c:c + 1], h2[:, c, :],
                                       start=c == 0, stop=c == HID2 // P - 1)
            ins.then_inc(s_yp, 1)

        @block.scalar
        def _(act):
            act.wait_ge(s_wchain, 14)
            for l in range(2):
                nc.scalar.activation(whi[l][:], raw[l], ACT.Copy, scale=wpow[:, 1:2]).then_inc(s_split, 1)

            act.wait_ge(s_setup, 6)

            def products(layer, t, n, parity, free):
                a = A_BANKS[layer].index(n)
                wait(act, s_y[layer], t * BANKS + n + 1)
                for w in free:
                    wait(act, *w)
                col = xc[:, parity, 1 - layer, :]
                for k in range(Q):
                    j = n * Q + k
                    nc.scalar.activation(prods[:, a, k * P:(k + 1) * P], ybank[n % RING][:, k * P:(k + 1) * P],
                                         ACT.Copy, scale=col[:, j:j + 1]).then_inc(s_prod[layer], 1)

            def free_of(layer, t, a):
                if a == 0:
                    return s_fma[layer], t * FMAS[layer] + Q
                return s_sum[layer], t * SUMS[layer] + FREED[layer][a]

            def x0_hi(t):
                wait(act, s_epi0, t * EPI0 + 4)
                wait(act, s_x0t, t)
                nc.scalar.activation(x0hl[:, 0:F], xx[:, bass.ds(t, 1), :].rearrange("p a f -> p (a f)"), ACT.Copy,
                                     scale=sc0[:]).then_inc(s_x0hi, 1)

            def save_x0(t):
                wait(act, s_x0t, t + 1)
                wait(act, s_zt, t * 3)
                nc.scalar.activation(x0T[:], misc[1][0:2 * F, 0:P // 2].bitcast(f16), ACT.Copy).then_inc(s_x0ts, 1)

            def freed(layer, t, other, other_t, a):
                if a < NA[layer] and active(t):
                    return [free_of(layer, t, a)]
                return [free_of(other, other_t, a)]

            def square_pairs(t, g):
                wait(act, s_zt, t * 3 + g + 1)
                if g == 0:
                    wait(act, s_l1, t)
                n = min(4, KT - 4 * g)
                nc.scalar.activation(zT[:, 4 * g:4 * g + n, :].rearrange("p t c -> p (t c)"),
                                     misc[PAIR_BANK[g]][:, 0:n * P], ACT.Square).then_inc(s_zts, 1)

            def hi_part(l, t):
                wait(act, s_epi[l], t * (EPI1, EPI2)[l] + (5, 8)[l])
                wait(act, s_xt[l], t)
                nc.scalar.activation(hi[l][:], r[l][:], ACT.Copy, scale=sc[l][:]).then_inc(s_hi[l], 1)

            def save_x(l, t):
                wait(act, s_xt[l], t + 1)
                wait(act, s_y[l], t * BANKS)
                nc.scalar.activation(xT[l][:].rearrange("p a c -> p (a c)"), misc[1][:, 0:P].bitcast(f16),
                                     ACT.Copy).then_inc(s_xts[l], 1)

            def step(v, parity):
                t1, t2, t3 = v + 2, v + 1, v
                wait(act, s_xc, v + 2)
                for n in range(2 * BANKS):
                    if n in A_BANKS[0] and active(t2):
                        products(0, t2, n, parity, freed(1, t3 - 1, 0, t2 - 1, A_BANKS[0].index(n)))
                    if n - BANKS in A_BANKS[1] and active(t3):
                        products(1, t3, n - BANKS, parity,
                                 freed(0, t2, 1, t3 - 1, A_BANKS[1].index(n - BANKS)))
                    if n == 0 and active(t1 + 1):
                        save_x0(t1 + 1)
                    if n == 12 and active(t1 + 2):
                        x0_hi(t1 + 2)
                    if n == 6 and active(t3):
                        save_x(1, t3)
                    if n == 9 and active(t1):
                        hi_part(0, t1)
                    if n in (12, 14, 21) and active(t1 + 1):
                        square_pairs(t1 + 1, (12, 14, 21).index(n))
                    if n == 19 and active(t1):
                        save_x(0, t1)
                    if n == 22 and active(t2):
                        hi_part(1, t2)

            steps(act, step)

            for i, c in enumerate(CHUNKS):
                k = F + CTX if c == 0 else P
                act.wait_ge(s_tt, i + 1)
                nc.scalar.activation(hT[0:k, c, :], ybank[TBANK[c]][0:k, :], ACT.Copy).then_inc(s_tts, 1)
            act.wait_ge(s_top, 8 * 16)
            h1bank = [misc[0], misc[1], ybank[3], ybank[4]]
            for m in range(HID1 // P):
                act.wait_ge(s_h1p, m + 1)
                nc.scalar.activation(h1[:, m, :], h1bank[m][:], ACT.Relu, bias=bt1_sb[:, m:m + 1]).then_inc(s_h1, 1)
            for m in range(HID2 // P):
                act.wait_ge(s_h2p, m + 1)
                nc.scalar.activation(h2[:, m, :], ybank[m][:], ACT.Relu, bias=bt2_sb[:, m:m + 1]).then_inc(s_h2, 1)
            act.wait_ge(s_yp, 1)
            nc.scalar.activation(y_sb[:], ybank[2][0:1, :], ACT.Copy).then_inc(s_ys, 1)

        @block.vector
        def _(dve):
            for l in range(2):
                for c in range(4):
                    dve.wait_ge(s_w[l][c], 16)
                    n = F * P // 4
                    nc.vector.tensor_reduce(wmax[:, 4 * l + c:4 * l + c + 1], raw[l][:, c * n:(c + 1) * n], axis=AX.X,
                                            op=ALU.max, apply_absolute_value=True).then_inc(s_wchain, 1)
            dve.wait_ge(s_wchain, 8)
            nc.vector.tensor_reduce(wmax[:, 8:9], wmax[:, 0:8], axis=AX.X, op=ALU.max).then_inc(s_wchain, 1)
            dve.wait_ge(s_wpe, 1)
            nc.vector.tensor_reduce(wmaxr[:, 0:1], misc[0][0:1, 0:P], axis=AX.X, op=ALU.max).then_inc(s_wchain, 1)
            dve.wait_ge(s_wchain, 10)
            nc.vector.tensor_scalar(wmaxr[:, 1:2], wmaxr[:, 0:1], TINY, HALF_RANGE, ALU.max, ALU.mult).then_inc(s_wchain, 1)
            dve.wait_ge(s_wchain, 11)
            nc.vector.tensor_scalar(wmaxr[:, 2:3].bitcast(u32), wmaxr[:, 1:2].bitcast(u32), EXPONENT, None,
                                    ALU.bitwise_and).then_inc(s_wchain, 1)
            dve.wait_ge(s_wpe, 2)
            nc.vector.tensor_copy(wpow[:, 0:1], misc[0][:, 0:1]).then_inc(s_wchain, 1)
            dve.wait_ge(s_wchain, 13)
            nc.vector.reciprocal(wpow[:, 1:2], wpow[:, 0:1]).then_inc(s_wchain, 1)
            dve.wait_ge(s_wpe, 3)
            nc.vector.tensor_copy(bcin[:].rearrange("p l o -> p (l o)"), misc[1][:, 0:3 * P]).then_inc(s_setup, 1)
            dve.wait_ge(s_in, 7 * 16)
            nc.vector.tensor_tensor(w1s[:], w1s[:], w1b[:], ALU.add).then_inc(s_setup, 1)
            dve.wait_ge(s_wchain, 14)
            for l in range(2):
                dve.wait_ge(s_split, l + 1)
                nc.vector.scalar_tensor_tensor(wlo[l][:], raw[l], wpow[:, 1:2], whi[l][:], ALU.mult,
                                               ALU.subtract).then_inc(s_setup, 1)
            dve.wait_ge(s_setup, 2)
            nc.vector.tensor_scalar(wsq[:], w1s[:], 0.5, None, ALU.mult).then_inc(s_setup, 1)
            dve.wait_ge(s_wpe, 4)
            dve.wait_ge(s_setup, 5)
            nc.vector.scalar_tensor_tensor(wsq[0:F, 0, :], misc[0][0:F, P:2 * P], -0.5, w1s[0:F, 0, :], ALU.mult,
                                           ALU.add).then_inc(s_setup, 1)
            dve.wait_ge(s_gather[0], 16 * F)
            for e0, e1 in ((0, 4), (4, E)):
                nc.vector.tensor_copy(xx[:, e0:e1, :], emb[:, 0, :, e0:e1].rearrange("p f e -> p e f")).then_inc(
                    s_xx, e1 - e0)

            def row(t):
                return xx[:, bass.ds(t, 1), :].rearrange("p a f -> p (a f)")

            def x0_scale(t, parity, i):
                s, done = s_epi0, t * EPI0
                if i == 0:
                    wait(dve, s_xx, t + 1)
                    nc.vector.tensor_reduce(mx0[:, 0:1], row(t), axis=AX.X, op=ALU.max,
                                            apply_absolute_value=True).then_inc(s, 1)
                elif i == 1:
                    wait(dve, s, done + 1)
                    nc.vector.tensor_scalar(mx0[:, 1:2], mx0[:, 0:1], TINY0, HALF_RANGE, ALU.max, ALU.mult).then_inc(s, 1)
                elif i == 2:
                    wait(dve, s, done + 2)
                    nc.vector.tensor_scalar(mp0[:].bitcast(u32), mx0[:, 1:2].bitcast(u32), EXPONENT, None,
                                            ALU.bitwise_and).then_inc(s, 1)
                elif i == 3:
                    wait(dve, s, done + 3)
                    wait(dve, s_x0hi, t)
                    nc.vector.reciprocal(sc0[:], mp0[:]).then_inc(s, 1)
                else:
                    nc.vector.tensor_tensor(msq[:, parity:parity + 1], mp0[:], mp0[:], ALU.mult).then_inc(s, 1)

            def x0_lo(t):
                wait(dve, s_x0hi, t + 1)
                wait(dve, s_x0t, t)
                wait(dve, s_epi0, t * EPI0 + 5)
                nc.vector.scalar_tensor_tensor(x0hl[:, F:2 * F], row(t), sc0[:], x0hl[:, 0:F], ALU.mult,
                                               ALU.subtract).then_inc(s_epi0, 1)

            def columns(v, parity):
                t3, t2 = v + 1, v + 2
                if not active(t3) and not active(t2):
                    return
                wait(dve, s_xx, (t2 if active(t2) else t3) + 1)
                wait(dve, s_prod[1], v * PRODS[1])
                wait(dve, s_prod[0], (v + 1) * PRODS[0])
                k0, k1 = (0 if active(t3) else 1), (2 if active(t2) else 1)
                nc.vector.tensor_scalar(xc[:, 1 - parity, k0:k1, :], xx[:, bass.ds(t3 + k0, k1 - k0), :],
                                        wpow[:, 0:1], None, ALU.mult).then_inc(s_xc, 1)

            def fma(layer, t, q, parity):
                n, k = D_BANKS[layer][q // Q], q % Q
                j = n * Q + k
                if k == 0:
                    wait(dve, s_y[layer], t * BANKS + n + 1)
                dst = acc[layer][:, k * P:(k + 1) * P]
                if q < Q:
                    wait(dve, s_prod[layer], t * PRODS[layer] + k + 1)
                    if k == 0:
                        wait(dve, s_epi[layer + 1], (t - 1) * (EPI2, EPI3)[layer] + 1)
                    add = prods[:, 0, k * P:(k + 1) * P]
                else:
                    wait(dve, s_fma[layer], t * FMAS[layer] + q - Q + 1)
                    add = dst
                nc.vector.scalar_tensor_tensor(dst, ybank[n % RING][:, k * P:(k + 1) * P],
                                               xc[:, parity, 1 - layer, j:j + 1], add, ALU.mult,
                                               ALU.add).then_inc(s_fma[layer], 1)

            def scale(l, t, parity, i, s, done):
                wait(dve, s, done + i)
                if i == 0:
                    nc.vector.tensor_scalar(mx[l][:, 1:2], mx[l][:, 0:1], TINY, HALF_RANGE, ALU.max,
                                            ALU.mult).then_inc(s, 1)
                elif i == 1:
                    nc.vector.tensor_scalar(mp[l][:, parity:parity + 1].bitcast(u32), mx[l][:, 1:2].bitcast(u32),
                                            EXPONENT, None, ALU.bitwise_and).then_inc(s, 1)
                else:
                    wait(dve, s_hi[l], t)
                    nc.vector.reciprocal(sc[l][:], mp[l][:, parity:parity + 1]).then_inc(s, 1)

            def relu_max(l, t, s, done):
                wait(dve, s, done)
                wait(dve, s_pool[l], t + 1)
                wait(dve, s_hi[l], t)
                nc.vector.tensor_scalar(r[l][:], pre[l][:], 0.0, None, ALU.max, ALU.max,
                                        accum_out=mx[l][:, 0:1]).then_inc(s, 1)

            def lo_part(l, t):
                n = (EPI1, EPI2)[l]
                wait(dve, s_hi[l], t + 1)
                wait(dve, s_xt[l], t)
                wait(dve, s_epi[l], t * n + n - 1)
                nc.vector.scalar_tensor_tensor(lo[l][:], r[l][:], sc[l][:], hi[l][:], ALU.mult,
                                               ALU.subtract).then_inc(s_epi[l], 1)

            def merge(layer, t, parity, i, s, done):
                if i == 0:
                    wait(dve, s_fma[layer], (t + 1) * FMAS[layer])
                    nc.vector.tensor_tensor(hs[layer][:], acc[layer][:, 0:2 * P], acc[layer][:, 2 * P:4 * P],
                                            ALU.add).then_inc(s, 1)
                elif i == 1:
                    wait(dve, s_sum[layer], (t + 1) * SUMS[layer])
                    wait(dve, s, done + 1)
                    nc.vector.tensor_tensor(hs[layer][:], hs[layer][:], half[layer][:], ALU.add).then_inc(s, 1)
                elif i == 2:
                    wait(dve, s, done + 2)
                    nc.vector.tensor_tensor(ssum[layer][:], hs[layer][:, 0:P], hs[layer][:, P:2 * P],
                                            ALU.add).then_inc(s, 1)
                else:
                    wait(dve, s, done + 3)
                    nc.vector.scalar_tensor_tensor(pre[layer + 1][:], ssum[layer][:], mp[layer][:, parity:parity + 1],
                                                   bcin[:, layer + 1, :], ALU.mult, ALU.add).then_inc(s, 1)

            def epilogue1(t, parity, i):
                s, done = s_epi[0], t * EPI1
                if i == 0:
                    wait(dve, s_l1, t + 1)
                    wait(dve, s_epi0, t * EPI0 + 5)
                    nc.vector.scalar_tensor_tensor(pre[0][:], misc[0][:, 0:P], msq[:, parity:parity + 1],
                                                   bcin[:, 0, :], ALU.mult, ALU.add).then_inc(s, 1)
                elif i == 1:
                    relu_max(0, t, s, done + 1)
                else:
                    scale(0, t, parity, i - 2, s, done + 2)

            def epilogue2(t, parity, i):
                s, done = s_epi[1], t * EPI2
                if i < 4:
                    merge(0, t, parity, i, s, done)
                elif i == 4:
                    relu_max(1, t, s, done + 4)
                else:
                    scale(1, t, parity, i - 5, s, done + 5)

            def epilogue3(t, parity, i):
                s, done = s_epi[2], t * EPI3
                if i < 4:
                    merge(1, t, parity, i, s, done)
                else:
                    wait(dve, s, done + 4)
                    wait(dve, s_pool[2], t + 1)
                    nc.vector.tensor_scalar(r[2][:], pre[2][:], 0.0, None, ALU.max).then_inc(s, 1)

            def x0_over_e(b):
                nc.vector.tensor_reduce(low[:, b, 0:F], emb[:, b, :, :], axis=AX.X, op=ALU.add).then_inc(s_low, 1)

            def step(v, parity):
                t1, t2, t3 = v + 2, v + 1, v
                other = 1 - parity
                wait(dve, s_xc, v + 2)
                if isinstance(v, int) and v == TILES - 1:
                    x0_over_e(NB - 1)
                for n in range(2 * BANKS):
                    layer, m = n // BANKS, n % BANKS
                    if m not in D_BANKS[layer]:
                        continue
                    for k in range(Q):
                        if active((t2, t3)[layer]):
                            fma(layer, (t2, t3)[layer], D_BANKS[layer].index(m) * Q + k, parity)
                        slot = n * Q + k
                        if 24 <= slot < 28 and active(t1):
                            epilogue1(t1, parity, slot - 24)
                        if slot == 32 and active(t1):
                            epilogue1(t1, parity, 4)
                        if 33 <= slot < 36 and active(t3 - 1):
                            epilogue3(t3 - 1, other, slot - 33)
                        if 40 <= slot < 42 and active(t3 - 1):
                            epilogue3(t3 - 1, other, slot - 37)
                        if 42 <= slot < 44 and active(t1 + 2):
                            x0_scale(t1 + 2, parity, slot - 42)
                        if slot == 68 and active(t2):
                            epilogue2(t2, other, 0)
                        if 76 <= slot < 80 and active(t2):
                            epilogue2(t2, other, slot - 75)
                        if 84 <= slot < 87 and active(t2):
                            epilogue2(t2, other, slot - 79)
                    if n == 10:
                        if active(t1 + 2):
                            for i in (2, 3, 4):
                                x0_scale(t1 + 2, parity, i)
                        if active(t1):
                            lo_part(0, t1)
                    if n == 13:
                        columns(v, parity)
                        if isinstance(v, int) and TILES - NB <= v < TILES - 1:
                            x0_over_e(v - TILES + NB)
                    if n == 15 and active(t1 + 2):
                        x0_lo(t1 + 2)
                if active(t2):
                    lo_part(1, t2)

            steps(dve, step)
            for i in range(EPI3):
                epilogue3(TILES - 1, 1, i)


def pair_rows():
    pairs = [(i, (i + d) % F) for d in range(SHIFTS) for i in range(F)][:PAIRS]
    first = np.array([i * F + j for i, j in pairs])
    second = np.array([j * F + i for i, j in pairs])
    return first, second


def kernel(**inputs):
    import concourse.bacc as bacc
    from concourse.bass_utils import run_bass_kernel_spmd

    nc = bacc.Bacc("TRN2", target_bir_lowering=False, num_devices=1)
    arrays = {}

    def given(name, a):
        a = np.ascontiguousarray(a)
        arrays[name] = a
        return nc.dram_tensor(name, a.shape, mybir.dt.from_np(a.dtype), kind="ExternalInput").ap()

    first, second = pair_rows()
    w1 = np.asarray(inputs["L0_rec_W1"])

    def by_tile(rows, off_diagonal):
        w = np.zeros((Z, P), w1.dtype)
        w[off_diagonal:PAIRS] = w1[rows[off_diagonal:]]
        return w.reshape(KT, P, P).transpose(1, 0, 2)

    members = np.zeros((F, Z), np.float16)
    members[first // F, np.arange(PAIRS)] = 1
    members[first % F, np.arange(PAIRS)] = 1
    distinct = members.astype(np.float32)
    distinct[:, :F] = 0

    ids = given("ids", inputs["ids"])
    tables = [given(f"tbl_{f}", inputs[f"tbl_{f}"]) for f in range(F)]
    args = [
        given("dense_ctx", inputs["dense_ctx"]),
        given("select", np.concatenate([members, members])),
        given("pairs_of", distinct.T.reshape(KT, P, F).transpose(1, 0, 2)),
        given("w_pair", by_tile(first, 0)),
        given("w_pair_t", by_tile(second, F)),
        given("w2", np.asarray(inputs["L0_rec_W2"]).reshape(P, F * P)),
        given("w3", np.asarray(inputs["L0_rec_W3"]).reshape(P, F * P)),
        [given(f"b{l}", inputs[f"L0_rec_b{l}"]) for l in (1, 2, 3)],
        given("W_top1", inputs["W_top1"]), given("b_top1", inputs["b_top1"]),
        given("W_top2", inputs["W_top2"]), given("b_top2", inputs["b_top2"]),
        given("W_top3", inputs["W_top3"]),
    ]
    out = nc.dram_tensor("out", (B, 1), mybir.dt.float32, kind="ExternalOutput").ap()
    build(nc, ids, tables, *args, out)
    result = run_bass_kernel_spmd(nc, [arrays], core_ids=[0])
    return result.results[0]["out"]
```

```python
from contextlib import ExitStack

import numpy as np

import concourse.bass as bass
import concourse.mybir as mybir

ROWS = [1000, 12500, 1000, 125000, 1000, 125000, 1000, 12500, 12500, 1000, 1000, 1000, 125000, 125000,
        1000, 1250, 125000, 12500, 1250, 125000, 1000, 1000, 1250, 125000, 12500, 1000, 12500, 12500,
        1000, 1000, 1000, 1000, 1250, 1000, 1000, 1000, 1250, 1000, 1250, 1000, 1250, 1250, 1000, 1000,
        1000, 1000, 1000, 1000]
F = len(ROWS)
E = 32
B = 512
P = 128
NB = B // P
TILES = NB * E
CTX = 16
SHIFTS = F // 2 + 1
PAIRS = F * (F + 1) // 2
KT = -(-PAIRS // P)
REST = PAIRS - (KT - 1) * P
COPIES = (0, 32, 64)
STACK = COPIES[-1] + REST
assert REST <= 32
SPLIT = range(4, 8)
Z = KT * P
Q = 4
BANKS = F // Q
RING = 6
HID1, HID2 = 512, 256

TAKES = ("ADADAADADADA", "ADADADADADAD")
A_BANKS = [[n for n in range(BANKS) if t[n] == "A"] for t in TAKES]
D_BANKS = [[n for n in range(BANKS) if t[n] == "D"] for t in TAKES]
NA = [len(a) for a in A_BANKS]
PRODS, FMAS = [Q * len(a) for a in A_BANKS], [Q * len(d) for d in D_BANKS]
SUMS = (7, 6)
FREED = ({1: 1, 2: 1, 3: 2, 4: 2, 5: 4, 6: 6}, {1: 1, 2: 1, 3: 2, 4: 2, 5: 5})
CHUNKS = (1, 2, 0, 3)
TBANK = {1: 0, 2: 1, 0: 2, 3: 5}
GATHERS, SPREAD = 3, 8
PAIR_BANK = (1, 0, 0)
SETUP = 11
EPI0 = 6
EPI1, EPI2, EPI3 = 6, 9, 5

HALF_RANGE = 2.0 ** -13
SQUARE = 2.0 ** -8
TINY = 1e-30
TINY0 = 1e-15
EXPONENT = 0x7F800000


def build(nc, ids, tables, ctx_in, select, pairs_of, w_pair, w_pair_t, w2, w3, b_cin, wt1, bt1, wt2, bt2, wt3, out):
    f32, f16, i32, u32 = mybir.dt.float32, mybir.dt.float16, mybir.dt.int32, mybir.dt.uint32
    ALU, ACT, AX = mybir.AluOpType, mybir.ActivationFunctionType, mybir.AxisListType

    with ExitStack() as stack:
        def sb(name, shape, dt=f32):
            return stack.enter_context(nc.sbuf_tensor(name, shape, dt))

        def ps(name, shape, dt=f32):
            return stack.enter_context(nc.psum_tensor(name, shape, dt))

        def sem(name):
            return stack.enter_context(nc.semaphore(name))

        def wait(eng, s, value):
            if not (isinstance(value, int) and value <= 0):
                eng.wait_ge(s, value)

        ids_sb = sb("ids_sb", [P, NB, F], i32)
        emb = sb("emb", [P, NB, F, E])
        xx = sb("xx", [P, TILES, F])
        work = sb("work", [P, F * P])
        prods = work[:, 0:max(NA) * Q * P].rearrange("p (a k o) -> p a (k o)", a=max(NA), k=Q)
        zT = work[:, max(NA) * Q * P:max(NA) * Q * P + Z].rearrange("p (t c) -> p t c", c=P)
        w1s = sb("w1s", [P, KT, P])
        w1b = sb("w1b", [P, KT, P])
        wsq = sb("wsq", [P, KT, P])
        zhl, whl = sb("zhl", [P, 2, len(SPLIT) * P], f16), sb("whl", [P, 2, len(SPLIT) * P], f16)
        wst, zst = sb("wst", [P, P], f16), sb("zst", [P, P], f16)
        sel = sb("sel", [2 * F, Z], f16)
        member = sb("member", [P, KT, F])
        x0hl = sb("x0hl", [P, 2 * F], f16)
        x0T = sb("x0T", [2 * F, P], f16)
        mx0, sc0 = sb("mx0", [P, 2]), sb("sc0", [P, 1])
        mp0, msq = sb("mp0", [P, 1]), sb("msq", [P, 2])
        whi = [sb(f"whi{l}", [P, F * P], f16) for l in (2, 3)]
        wlo = [sb(f"wlo{l}", [P, F * P], f16) for l in (2, 3)]
        bcin = sb("bcin", [P, 3, P])
        brow = sb("brow", [1, 3 * P])
        ones = sb("ones", [1, P])
        eye32 = sb("eye32", [P, P])
        eye16 = sb("eye16", [P, P], f16)
        wmax = sb("wmax", [P, 16])
        wmaxr = sb("wmaxr", [1, 6])
        wpow, winv = sb("wpow", [P, 2]), sb("winv", [P, 2])
        zunit = sb("zunit", [P, 1])
        xc = sb("xc", [P, 2, 2, F])
        hi = [sb(f"hi{l}", [P, P], f16) for l in (1, 2)]
        lo = [sb(f"lo{l}", [P, P], f16) for l in (1, 2)]
        xT = [sb(f"xT{l}", [P, 2, P], f16) for l in (1, 2)]
        acc = [sb(f"acc{l}", [P, Q * P]) for l in (2, 3)]
        part = sb("part", [P, 2, Q * P])
        half = [sb(f"half{l}", [P, 2 * P]) for l in (2, 3)]
        hs = [sb(f"hs{l}", [P, 2 * P]) for l in (2, 3)]
        ssum = [sb(f"ssum{l}", [P, P]) for l in (2, 3)]
        pre = [sb(f"pre{l}", [P, P]) for l in (1, 2, 3)]
        r = [sb(f"r{l}", [P, P]) for l in (1, 2, 3)]
        mx = [sb(f"mx{l}", [P, 2]) for l in (1, 2)]
        mp = [sb(f"mp{l}", [P, 2]) for l in (1, 2)]
        sc = [sb(f"sc{l}", [P, 1]) for l in (1, 2)]
        pooled = sb("pooled", [P, NB, 3, P])
        low = sb("low", [P, NB, F + CTX])
        hT = sb("hT", [P, 4, B])
        wt1_sb = sb("wt1_sb", [P, 4, HID1])
        wt2_sb = sb("wt2_sb", [P, HID1 // P, HID2])
        wt3_sb = sb("wt3_sb", [P, HID2 // P])
        bt1_sb = sb("bt1_sb", [P, HID1 // P])
        bt2_sb = sb("bt2_sb", [P, HID2 // P])
        y_sb = sb("y_sb", [1, B])
        flat = xx[:].rearrange("p t w -> p (t w)")
        h1 = flat[:, 0:4 * B].rearrange("p (c n) -> p c n", n=B)
        h2 = flat[:, 4 * B:6 * B].rearrange("p (c n) -> p c n", n=B)
        raw = [flat, work[:]]

        ybank = [ps(f"y{n}", [P, Q * P]) for n in range(RING)]
        misc = [ps(f"m{n}", [P, Q * P]) for n in range(2)]

        s_ids, s_in, s_top = sem("ids_loaded"), sem("small_loaded"), sem("top_loaded")
        s_w = [[sem(f"w{l}_{c}_loaded") for c in range(4)] for l in (2, 3)]
        s_gather = [sem(f"gathered{b}") for b in range(NB)]
        s_const = sem("constants_ready")
        s_wchain, s_wpe, s_split = sem("weight_scale_steps"), sem("weight_scale_pe"), sem("weights_hi")
        s_setup = sem("setup_done")
        s_xx = sem("xx_tiles")
        s_epi0, s_x0hi = sem("x0_steps"), sem("x0_hi")
        s_x0t, s_x0ts = sem("x0T_in_psum"), sem("x0T_saved")
        s_zt, s_zts = sem("pair_sums_in_psum"), sem("squares_saved")
        s_zhi, s_zlo, s_zst = sem("squares_hi"), sem("squares_lo"), sem("stacked_squares_ready")
        s_l1 = sem("layer1_in_psum")
        s_epi = [sem(f"epilogue{l}_steps") for l in (1, 2, 3)]
        s_hi = [sem(f"hi{l}_ready") for l in (1, 2)]
        s_xt, s_xts = [sem(f"xT{l}_in_psum") for l in (1, 2)], [sem(f"xT{l}_saved") for l in (1, 2)]
        s_y = [sem(f"y{l}_ready") for l in (2, 3)]
        s_prod = [sem(f"products{l}") for l in (2, 3)]
        s_fma = [sem(f"fmas{l}") for l in (2, 3)]
        s_sum = [sem(f"sums{l}") for l in (2, 3)]
        s_pool = [sem(f"pooled{l}") for l in (1, 2, 3)]
        s_xc = sem("xc_ready")
        s_tt, s_tts, s_low, s_h1p, s_h1, s_h2p, s_h2, s_yp, s_ys, s_out = (
            sem(n) for n in ("hT_in_psum", "hT_saved", "low_ready", "h1_in_psum", "h1_ready", "h2_in_psum",
                             "h2_ready", "y_in_psum", "y_saved", "y_stored"))

        def bank_done(eng, layer, tile, n):
            if n in A_BANKS[layer]:
                wait(eng, s_prod[layer], tile * PRODS[layer] + Q * (A_BANKS[layer].index(n) + 1))
            else:
                wait(eng, s_fma[layer], tile * FMAS[layer] + Q * (D_BANKS[layer].index(n) + 1))

        def steps(eng, step):
            for v in range(-4, 1):
                step(v, v % 2)
            with eng.Fori(0, (TILES - 6) // 2) as pair:
                step(pair * 2 + 1, 1)
                step(pair * 2 + 2, 0)
            for v in range(TILES - 5, TILES):
                step(v, v % 2)

        def active(tile):
            return not isinstance(tile, int) or 0 <= tile < TILES

        block = stack.enter_context(nc.Block())

        @block.sync
        def _(sp):
            sp.dma_start(ids_sb[:], ids.rearrange("(b p) f -> p b f", p=P)).then_inc(s_ids, 16)
            sp.dma_start(w1s[:], w_pair).then_inc(s_in, 16)
            sp.dma_start(w1b[:], w_pair_t).then_inc(s_in, 16)
            sp.dma_start(sel[:], select).then_inc(s_in, 16)
            sp.dma_start(member[:], pairs_of).then_inc(s_in, 16)
            for l in range(3):
                sp.dma_start(brow[:, l * P:(l + 1) * P], b_cin[l].rearrange("(a n) -> a n", a=1)).then_inc(s_in, 16)
            for l, w in enumerate((w2, w3)):
                for c in range(4):
                    n = F * P // 4
                    sp.dma_start(raw[l][:, c * n:(c + 1) * n], w[:, c * n:(c + 1) * n]).then_inc(s_w[l][c], 16)
            sp.dma_start(low[:, :, F:F + CTX], ctx_in.rearrange("(b p) c -> p b c", p=P)).then_inc(s_top, 16)
            sp.dma_start(wt1_sb[0:F, 0, :], wt1[0:F, :]).then_inc(s_top, 16)
            sp.dma_start(wt1_sb[F:F + CTX, 0, :], wt1[F + 3 * P:F + 3 * P + CTX, :]).then_inc(s_top, 16)
            sp.dma_start(wt1_sb[:, 1:4, :], wt1[F:F + 3 * P, :].rearrange("(c p) n -> p c n", p=P)).then_inc(s_top, 16)
            sp.dma_start(wt2_sb[:], wt2.rearrange("(c p) n -> p c n", p=P)).then_inc(s_top, 16)
            with nc.allow_non_contiguous_dma(reason="a few hundred bias and weight scalars"):
                sp.dma_start(wt3_sb[:], wt3.rearrange("(c p) n -> p (c n)", p=P)).then_inc(s_top, 16)
                sp.dma_start(bt1_sb[:], bt1.rearrange("(c p) -> p c", p=P)).then_inc(s_top, 16)
                sp.dma_start(bt2_sb[:], bt2.rearrange("(c p) -> p c", p=P)).then_inc(s_top, 16)
            sp.wait_ge(s_ys, 1)
            sp.dma_start(out.rearrange("n a -> a n"), y_sb[:]).then_inc(s_out, 16)
            sp.wait_ge(s_out, 16)

        @block.gpsimd
        def _(pool):
            def gather(b, fields):
                for f in fields:
                    pool.indirect_dma_start(
                        emb[:, b, f, :], None, tables[f],
                        bass.IndirectOffsetOnAxis(ap=ids_sb[:, b, f:f + 1], axis=0)).then_inc(s_gather[b], 16)

            def spread(b, e0, n):
                t0 = b * E + e0
                src = emb[:, b, :, e0:e0 + n].rearrange("p f e -> p e f")
                pool.wait_ge(s_gather[b], 16 * F)
                pool.tensor_copy(xx[:, t0:t0 + n, :], src).then_inc(s_xx, n)

            pool.memset(eye32[:], 0.0).then_inc(s_const, 1)
            pool.memset(eye16[:], 0.0).then_inc(s_const, 1)
            pool.memset(ones[:], 1.0).then_inc(s_const, 1)
            pool.wait_ge(s_const, 3)
            for m in (eye32, eye16):
                pool.affine_select(out=m[:], in_=m[:], compare_op=ALU.not_equal, fill=1.0, base=0,
                                   pattern=[[-1, P]], channel_multiplier=1).then_inc(s_const, 1)
            pool.wait_ge(s_ids, 16)
            gather(0, range(F))
            for l in range(3):
                pool.memset(pooled[:, :, l, :], 0.0).then_inc(s_pool[l], 1)

            def sums(layer, tile, first):
                s, done = s_sum[layer], tile * SUMS[layer]
                a, b = part[:, 0, :], part[:, 1, :]

                def add(o, x, y):
                    pool.tensor_tensor(o, x, y, ALU.add).then_inc(s, 1)

                def written(m):
                    wait(pool, s_prod[layer], tile * PRODS[layer] + (m + 1) * Q)

                for w in first:
                    wait(pool, *w)
                written(2)
                add(a, prods[:, 1, :], prods[:, 2, :])
                written(4)
                add(b, prods[:, 3, :], prods[:, 4, :])
                wait(pool, s, done + 2)
                add(a, a, b)
                n = 3
                if NA[layer] == 7:
                    written(5)
                    wait(pool, s, done + 3)
                    add(a, a, prods[:, 5, :])
                    n = 4
                wait(pool, s, done + n)
                wait(pool, s_epi[layer + 1], (tile - 1) * (EPI2, EPI3)[layer] + 2)
                add(half[layer][:], a[:, 0:2 * P], a[:, 2 * P:4 * P])
                last = NA[layer] - 1
                written(last)
                add(b[:, 0:2 * P], prods[:, last, 0:2 * P], prods[:, last, 2 * P:4 * P])
                wait(pool, s, done + n + 2)
                add(half[layer][:], half[layer][:], b[:, 0:2 * P])

            def over_e(l, tile, block_of, value):
                if not active(tile):
                    return
                wait(pool, s_epi[l], value)
                wait(pool, s_pool[l], tile + 1)
                dst = pooled[:, block_of, l, :]
                pool.tensor_tensor(dst, dst, r[l][:], ALU.add).then_inc(s_pool[l], 1)

            def step(v, b1, b2, b3, fields=(), columns=None):
                over_e(1, v, b2, v * EPI2 + 5)
                gather(b1 + 1, fields[0:1])
                if active(v + 1):
                    sums(0, v + 1, [(s_sum[1], v * SUMS[1])] if active(v) else [])
                gather(b1 + 1, fields[1:2])
                if columns:
                    spread(b1 + 1, *columns)
                over_e(2, v - 1, b3, (v - 1) * EPI3 + 5)
                if active(v):
                    sums(1, v, [(s_sum[0], (v + 2) * SUMS[0])] if active(v + 1) else [])
                gather(b1 + 1, fields[2:3])
                over_e(0, v + 2, b1, (v + 2) * EPI1 + 2)

            def run(v0, v1, b):
                with pool.Fori(v0, v1) as v:
                    step(v, b, b, b)

            for v in range(-4, 1):
                step(v, 0, 0, 0)
            for b in range(NB):
                v0, end = b * E + 1, (b + 1) * E - 2
                if b + 1 < NB:
                    for f in range(0, F, GATHERS):
                        step(v0, b, b, b, fields=range(f, f + GATHERS))
                        v0 += 1
                    for e in range(0, E, SPREAD):
                        step(v0, b, b, b, columns=(e, SPREAD))
                        v0 += 1
                run(v0, end, b)
                step(end, b + 1, b, b)
                step(end + 1, b + 1, b, b)
                if b + 1 < NB:
                    step(end + 2, b + 1, b + 1, b)
            over_e(2, TILES - 1, NB - 1, TILES * EPI3)

        @block.tensor
        def _(pe):
            pe.wait_ge(s_const, 5)
            pe.wait_ge(s_in, 7 * 16)
            nc.tensor.matmul(misc[1][:, 0:3 * P], ones[:], brow[:], start=True, stop=True).then_inc(s_wpe, 1)
            pe.wait_ge(s_setup, 1)
            for k in range(KT):
                ins = nc.tensor.matmul(misc[0][0:F, 0:P], member[:, k, :], w1s[:, k, :], start=k == 0, stop=k == KT - 1)
            ins.then_inc(s_wpe, 1)
            pe.wait_ge(s_wchain, 10)
            for g in range(2):
                ins = nc.tensor.transpose(misc[0][0:1, g * P:(g + 1) * P], wmax[:, 8 + g:9 + g], eye32[:])
            ins.then_inc(s_wpe, 1)
            pe.wait_ge(s_wchain, 13)
            nc.tensor.matmul(misc[0][:, 0:2], ones[:], wmaxr[:, 4:6], start=True, stop=True).then_inc(s_wpe, 1)
            pe.wait_ge(s_setup, SETUP)

            def transpose_x0(t):
                wait(pe, s_epi0, (t + 1) * EPI0)
                wait(pe, s_x0hi, t + 1)
                wait(pe, s_xts[0], t - 1)
                nc.tensor.transpose(misc[1][0:2 * F, 0:P // 2].bitcast(f16), x0hl[:], eye16[:]).then_inc(s_x0t, 1)

            def pair_sums(t, g):
                if g == 0:
                    wait(pe, s_x0ts, t + 1)
                    wait(pe, s_xts[1], t - 2)
                elif g == 1:
                    wait(pe, s_epi[0], (t - 1) * EPI1 + 1)
                else:
                    wait(pe, s_zts, t * 3 + 2)
                for k in range(4 * g, min(4 * g + 4, KT)):
                    ins = nc.tensor.matmul(misc[PAIR_BANK[g]][:, (k % 4) * P:(k % 4 + 1) * P],
                                           sel[:, k * P:(k + 1) * P], x0T[:], start=True, stop=True)
                ins.then_inc(s_zt, 1)

            def layer1(t, c):
                if c == 0:
                    wait(pe, s_zts, t * 3 + 3)
                for k in (2 * c, 2 * c + 1):
                    if k in SPLIT:
                        if k == SPLIT[0]:
                            wait(pe, s_zlo, t + 1)
                        cols = slice((k - SPLIT[0]) * P, (k - SPLIT[0] + 1) * P)
                        for a, w in ((0, 0), (0, 1), (1, 0)):
                            nc.tensor.matmul(misc[0][:, 0:P], zhl[:, a, cols], whl[:, w, cols], start=False, stop=False)
                    elif k < KT - 1:
                        nc.tensor.matmul(misc[0][:, 0:P], zT[:, k, :], wsq[:, k, :], start=k == 0, stop=False)
                    else:
                        wait(pe, s_zst, t + 1)
                        ins = nc.tensor.matmul(misc[0][:, 0:P], zst[0:STACK, :], wst[0:STACK, :], start=False, stop=True)
                if 2 * c + 2 == KT:
                    ins.then_inc(s_l1, 1)

            def transpose_x(l, t):
                wait(pe, s_hi[l], t + 1)
                wait(pe, s_epi[l], (t + 1) * (EPI1, EPI2)[l])
                dst = misc[1][:, 0:P].bitcast(f16)
                nc.tensor.transpose(dst[:, 0:P], hi[l][:], eye16[:])
                nc.tensor.transpose(dst[:, P:2 * P], lo[l][:], eye16[:]).then_inc(s_xt[l], 1)

            def y_item(layer, t, n):
                if n == 0:
                    wait(pe, s_xts[layer], t + 1)
                dst = ybank[n % RING]
                cols = slice(n * Q * P, (n + 1) * Q * P)
                for m, (a, w) in enumerate(((0, whi), (0, wlo), (1, whi))):
                    ins = nc.tensor.matmul(dst[:], xT[layer][:, a, :], w[layer][:, cols], start=m == 0, stop=m == 2)
                ins.then_inc(s_y[layer], 1)

            def step(v, parity):
                t0, t1, t2, t3 = v + 3, v + 2, v + 1, v
                for n in range(2 * BANKS):
                    if n == 0 and active(t0):
                        transpose_x0(t0)
                    if n in (12, 14, 21) and active(t0):
                        pair_sums(t0, (12, 14, 21).index(n))
                    if 3 <= n < 8 and active(t1):
                        layer1(t1, n - 3)
                    if n == 6 and active(t3):
                        if active(t0):
                            wait(pe, s_x0ts, t0 + 1)
                        elif active(t2):
                            wait(pe, s_xts[0], t2 + 1)
                        else:
                            wait(pe, s_xts[1], t3)
                        transpose_x(1, t3)
                    if n == 18 and active(t1):
                        if active(t0):
                            wait(pe, s_zts, t0 * 3 + 1)
                        else:
                            wait(pe, s_xts[1], t3 + 1)
                        transpose_x(0, t1)
                    m = n % BANKS
                    if n < BANKS and active(t2):
                        if m >= RING:
                            bank_done(pe, 0, t2, m - RING)
                        elif active(t3 - 1):
                            bank_done(pe, 1, t3 - 1, m + RING)
                        else:
                            bank_done(pe, 0, t2 - 1, m + RING)
                        y_item(0, t2, m)
                    if n >= BANKS and active(t3):
                        if m >= RING:
                            bank_done(pe, 1, t3, m - RING)
                        elif active(t2):
                            bank_done(pe, 0, t2, m + RING)
                        else:
                            bank_done(pe, 1, t3 - 1, m + RING)
                        y_item(1, t3, m)

            steps(pe, step)

            last = TILES - 1
            pe.wait_ge(s_top, 8 * 16)
            for l in (0, 1):
                pe.wait_ge(s_pool[l], TILES + 1)
                bank_done(pe, 1, last, RING + TBANK[l + 1])
                for b in range(NB):
                    ins = nc.tensor.transpose(ybank[TBANK[l + 1]][:, b * P:(b + 1) * P], pooled[:, b, l, :], eye32[:])
                ins.then_inc(s_tt, 1)
            pe.wait_ge(s_low, NB)
            bank_done(pe, 1, last, RING + TBANK[0])
            for b in range(NB):
                ins = nc.tensor.transpose(ybank[TBANK[0]][0:F + CTX, b * P:(b + 1) * P], low[:, b, :], eye32[:])
            ins.then_inc(s_tt, 1)
            wait(pe, s_epi[0], TILES * EPI1)
            wait(pe, s_xts[1], TILES)
            h1bank = [misc[0], misc[1], ybank[3], ybank[4]]
            bank_done(pe, 1, last, RING + 3)
            bank_done(pe, 1, last, RING + 4)
            for i, c in enumerate(CHUNKS):
                if i == 2:
                    pe.wait_ge(s_pool[2], TILES + 1)
                    bank_done(pe, 1, last, RING + TBANK[3])
                    for b in range(NB):
                        ins = nc.tensor.transpose(ybank[TBANK[3]][:, b * P:(b + 1) * P], pooled[:, b, 2, :], eye32[:])
                    ins.then_inc(s_tt, 1)
                pe.wait_ge(s_tts, i + 1)
                k = F + CTX if c == 0 else P
                for m in range(HID1 // P):
                    ins = nc.tensor.matmul(h1bank[m][:], wt1_sb[0:k, c, m * P:(m + 1) * P], hT[0:k, c, :],
                                           start=i == 0, stop=c == 3)
                    if c == 3:
                        ins.then_inc(s_h1p, 1)
            for c in range(HID1 // P):
                pe.wait_ge(s_h1, c + 1)
                for m in range(HID2 // P):
                    ins = nc.tensor.matmul(ybank[m][:], wt2_sb[:, c, m * P:(m + 1) * P], h1[:, c, :],
                                           start=c == 0, stop=c == HID1 // P - 1)
                    if c == HID1 // P - 1:
                        ins.then_inc(s_h2p, 1)
            for c in range(HID2 // P):
                pe.wait_ge(s_h2, c + 1)
                ins = nc.tensor.matmul(ybank[2][0:1, :], wt3_sb[:, c:c + 1], h2[:, c, :],
                                       start=c == 0, stop=c == HID2 // P - 1)
            ins.then_inc(s_yp, 1)

        @block.scalar
        def _(act):
            act.wait_ge(s_wchain, 15)
            for l in range(2):
                nc.scalar.activation(whi[l][:], raw[l], ACT.Copy, scale=winv[:, 0:1]).then_inc(s_split, 1)

            act.wait_ge(s_setup, SETUP)

            def products(layer, t, n, parity, free):
                a = A_BANKS[layer].index(n)
                wait(act, s_y[layer], t * BANKS + n + 1)
                for w in free:
                    wait(act, *w)
                col = xc[:, parity, 1 - layer, :]
                for k in range(Q):
                    j = n * Q + k
                    nc.scalar.activation(prods[:, a, k * P:(k + 1) * P], ybank[n % RING][:, k * P:(k + 1) * P],
                                         ACT.Copy, scale=col[:, j:j + 1]).then_inc(s_prod[layer], 1)

            def free_of(layer, t, a):
                if a == 0:
                    return s_fma[layer], t * FMAS[layer] + Q
                return s_sum[layer], t * SUMS[layer] + FREED[layer][a]

            def x0_hi(t):
                wait(act, s_epi0, t * EPI0 + 4)
                wait(act, s_x0t, t)
                nc.scalar.activation(x0hl[:, 0:F], xx[:, bass.ds(t, 1), :].rearrange("p a f -> p (a f)"), ACT.Copy,
                                     scale=sc0[:]).then_inc(s_x0hi, 1)

            def save_x0(t):
                wait(act, s_x0t, t + 1)
                wait(act, s_zt, t * 3)
                nc.scalar.activation(x0T[:], misc[1][0:2 * F, 0:P // 2].bitcast(f16), ACT.Copy).then_inc(s_x0ts, 1)

            def freed(layer, t, other, other_t, a):
                if a < NA[layer] and active(t):
                    return [free_of(layer, t, a)]
                return [free_of(other, other_t, a)]

            def square_pairs(t, g):
                wait(act, s_zt, t * 3 + g + 1)
                if g == 0:
                    wait(act, s_l1, t)
                n = min(4, KT - 4 * g)
                if 4 * g + n == KT:
                    nc.scalar.activation(zst[0:STACK, :], misc[PAIR_BANK[g]][0:STACK, (n - 1) * P:n * P], ACT.Square,
                                         scale=SQUARE)
                nc.scalar.activation(zT[:, 4 * g:4 * g + n, :].rearrange("p t c -> p (t c)"),
                                     misc[PAIR_BANK[g]][:, 0:n * P], ACT.Square, scale=SQUARE).then_inc(s_zts, 1)

            def squares_hi(t):
                wait(act, s_zts, t * 3 + 2)
                wait(act, s_l1, t)
                nc.scalar.activation(zhl[:, 0, :], zT[:, SPLIT[0]:SPLIT[-1] + 1, :].rearrange("p t c -> p (t c)"),
                                     ACT.Copy).then_inc(s_zhi, 1)

            def hi_part(l, t):
                wait(act, s_epi[l], t * (EPI1, EPI2)[l] + (5, 8)[l])
                wait(act, s_xt[l], t)
                nc.scalar.activation(hi[l][:], r[l][:], ACT.Copy, scale=sc[l][:]).then_inc(s_hi[l], 1)

            def save_x(l, t):
                wait(act, s_xt[l], t + 1)
                wait(act, s_y[l], t * BANKS)
                nc.scalar.activation(xT[l][:].rearrange("p a c -> p (a c)"), misc[1][:, 0:P].bitcast(f16),
                                     ACT.Copy).then_inc(s_xts[l], 1)

            def step(v, parity):
                t1, t2, t3 = v + 2, v + 1, v
                wait(act, s_xc, v + 2)
                for n in range(2 * BANKS):
                    if n in A_BANKS[0] and active(t2):
                        products(0, t2, n, parity, freed(1, t3 - 1, 0, t2 - 1, A_BANKS[0].index(n)))
                    if n - BANKS in A_BANKS[1] and active(t3):
                        products(1, t3, n - BANKS, parity,
                                 freed(0, t2, 1, t3 - 1, A_BANKS[1].index(n - BANKS)))
                    if n == 0 and active(t1 + 1):
                        save_x0(t1 + 1)
                    if n == 12 and active(t1 + 2):
                        x0_hi(t1 + 2)
                    if n == 6 and active(t3):
                        save_x(1, t3)
                    if n == 9 and active(t1):
                        hi_part(0, t1)
                    if n in (12, 14, 21) and active(t1 + 1):
                        square_pairs(t1 + 1, (12, 14, 21).index(n))
                    if n == 16 and active(t1 + 1):
                        squares_hi(t1 + 1)
                    if n == 19 and active(t1):
                        save_x(0, t1)
                    if n == 22 and active(t2):
                        hi_part(1, t2)

            steps(act, step)

            for i, c in enumerate(CHUNKS):
                k = F + CTX if c == 0 else P
                act.wait_ge(s_tt, i + 1)
                nc.scalar.activation(hT[0:k, c, :], ybank[TBANK[c]][0:k, :], ACT.Copy).then_inc(s_tts, 1)
            act.wait_ge(s_top, 8 * 16)
            h1bank = [misc[0], misc[1], ybank[3], ybank[4]]
            for m in range(HID1 // P):
                act.wait_ge(s_h1p, m + 1)
                nc.scalar.activation(h1[:, m, :], h1bank[m][:], ACT.Relu, bias=bt1_sb[:, m:m + 1]).then_inc(s_h1, 1)
            for m in range(HID2 // P):
                act.wait_ge(s_h2p, m + 1)
                nc.scalar.activation(h2[:, m, :], ybank[m][:], ACT.Relu, bias=bt2_sb[:, m:m + 1]).then_inc(s_h2, 1)
            act.wait_ge(s_yp, 1)
            nc.scalar.activation(y_sb[:], ybank[2][0:1, :], ACT.Copy).then_inc(s_ys, 1)

        @block.vector
        def _(dve):
            dve.wait_ge(s_in, 7 * 16)
            nc.vector.tensor_tensor(w1s[:], w1s[:], w1b[:], ALU.add).then_inc(s_setup, 1)
            dve.wait_ge(s_setup, 1)
            nc.vector.tensor_scalar(wsq[:], w1s[:], 0.5, None, ALU.mult).then_inc(s_setup, 1)
            dve.wait_ge(s_wpe, 2)
            dve.wait_ge(s_setup, 2)
            nc.vector.scalar_tensor_tensor(wsq[0:F, 0, :], misc[0][0:F, 0:P], -0.5, w1s[0:F, 0, :], ALU.mult,
                                           ALU.add).then_inc(s_setup, 1)
            for l in range(2):
                for c in range(4):
                    dve.wait_ge(s_w[l][c], 16)
                    n = F * P // 4
                    nc.vector.tensor_reduce(wmax[:, 4 * l + c:4 * l + c + 1], raw[l][:, c * n:(c + 1) * n], axis=AX.X,
                                            op=ALU.max, apply_absolute_value=True).then_inc(s_wchain, 1)
            dve.wait_ge(s_setup, 3)
            nc.vector.tensor_reduce(wmax[:, 9:10], wsq[:].rearrange("p t o -> p (t o)"), axis=AX.X, op=ALU.max,
                                    apply_absolute_value=True).then_inc(s_wchain, 1)
            dve.wait_ge(s_wchain, 8)
            nc.vector.tensor_reduce(wmax[:, 8:9], wmax[:, 0:8], axis=AX.X, op=ALU.max).then_inc(s_wchain, 1)
            dve.wait_ge(s_wpe, 3)
            nc.vector.tensor_reduce(wmaxr[:, 0:2], misc[0][0:1, 0:2 * P].rearrange("p (g n) -> p g n", g=2), axis=AX.X,
                                    op=ALU.max).then_inc(s_wchain, 1)
            dve.wait_ge(s_wchain, 11)
            nc.vector.tensor_scalar(wmaxr[:, 2:4], wmaxr[:, 0:2], TINY, HALF_RANGE, ALU.max, ALU.mult).then_inc(s_wchain, 1)
            dve.wait_ge(s_wchain, 12)
            nc.vector.tensor_scalar(wmaxr[:, 4:6].bitcast(u32), wmaxr[:, 2:4].bitcast(u32), EXPONENT, None,
                                    ALU.bitwise_and).then_inc(s_wchain, 1)
            dve.wait_ge(s_wpe, 4)
            nc.vector.tensor_copy(wpow[:], misc[0][:, 0:2]).then_inc(s_wchain, 1)
            dve.wait_ge(s_wchain, 14)
            nc.vector.reciprocal(winv[:], wpow[:]).then_inc(s_wchain, 1)
            nc.vector.tensor_scalar(zunit[:], wpow[:, 1:2], SQUARE ** -2, None, ALU.mult).then_inc(s_wchain, 1)
            dve.wait_ge(s_wpe, 1)
            nc.vector.tensor_copy(bcin[:].rearrange("p l o -> p (l o)"), misc[1][:, 0:3 * P]).then_inc(s_setup, 1)
            dve.wait_ge(s_wchain, 16)
            nc.vector.tensor_scalar(wsq[:], wsq[:], winv[:, 1:2], None, ALU.mult).then_inc(s_setup, 1)
            dve.wait_ge(s_setup, 5)
            nc.vector.tensor_copy(wst[:], wsq[:, KT - 1, :]).then_inc(s_setup, 1)
            w_split = wsq[:, SPLIT[0]:SPLIT[-1] + 1, :].rearrange("p t c -> p (t c)")
            nc.vector.tensor_copy(whl[:, 0, :], w_split).then_inc(s_setup, 1)
            dve.wait_ge(s_setup, 7)
            nc.vector.tensor_tensor(whl[:, 1, :], w_split, whl[:, 0, :], ALU.subtract).then_inc(s_setup, 1)
            rows = slice(COPIES[2], COPIES[2] + REST)
            nc.vector.tensor_tensor(wst[rows, :], wsq[rows, KT - 1, :], wst[rows, :], ALU.subtract).then_inc(s_setup, 1)
            for l in range(2):
                dve.wait_ge(s_split, l + 1)
                nc.vector.scalar_tensor_tensor(wlo[l][:], raw[l], winv[:, 0:1], whi[l][:], ALU.mult,
                                               ALU.subtract).then_inc(s_setup, 1)
            dve.wait_ge(s_gather[0], 16 * F)
            dve.wait_ge(s_setup, SETUP)
            for e0, e1 in ((0, 4), (4, E)):
                nc.vector.tensor_copy(xx[:, e0:e1, :], emb[:, 0, :, e0:e1].rearrange("p f e -> p e f")).then_inc(
                    s_xx, e1 - e0)

            def row(t):
                return xx[:, bass.ds(t, 1), :].rearrange("p a f -> p (a f)")

            def x0_scale(t, parity, i):
                s, done = s_epi0, t * EPI0
                if i == 0:
                    wait(dve, s_xx, t + 1)
                    nc.vector.tensor_reduce(mx0[:, 0:1], row(t), axis=AX.X, op=ALU.max,
                                            apply_absolute_value=True).then_inc(s, 1)
                elif i == 1:
                    wait(dve, s, done + 1)
                    nc.vector.tensor_scalar(mx0[:, 1:2], mx0[:, 0:1], TINY0, HALF_RANGE, ALU.max, ALU.mult).then_inc(s, 1)
                elif i == 2:
                    wait(dve, s, done + 2)
                    nc.vector.tensor_scalar(mp0[:].bitcast(u32), mx0[:, 1:2].bitcast(u32), EXPONENT, None,
                                            ALU.bitwise_and).then_inc(s, 1)
                elif i == 3:
                    wait(dve, s, done + 3)
                    wait(dve, s_x0hi, t)
                    nc.vector.reciprocal(sc0[:], mp0[:]).then_inc(s, 1)
                else:
                    nc.vector.scalar_tensor_tensor(msq[:, parity:parity + 1], mp0[:], zunit[:], mp0[:], ALU.mult,
                                                   ALU.mult).then_inc(s, 1)

            def x0_lo(t):
                wait(dve, s_x0hi, t + 1)
                wait(dve, s_x0t, t)
                wait(dve, s_epi0, t * EPI0 + 5)
                nc.vector.scalar_tensor_tensor(x0hl[:, F:2 * F], row(t), sc0[:], x0hl[:, 0:F], ALU.mult,
                                               ALU.subtract).then_inc(s_epi0, 1)

            def squares_lo(t):
                wait(dve, s_zhi, t + 1)
                nc.vector.tensor_tensor(zhl[:, 1, :], zT[:, SPLIT[0]:SPLIT[-1] + 1, :].rearrange("p t c -> p (t c)"),
                                        zhl[:, 0, :], ALU.subtract).then_inc(s_zlo, 1)

            def stacked_lo(t):
                rows = slice(COPIES[1], COPIES[1] + REST)
                wait(dve, s_zts, t * 3 + 3)
                nc.vector.tensor_tensor(zst[rows, :], zT[rows, KT - 1, :], zst[rows, :], ALU.subtract).then_inc(s_zst, 1)

            def columns(v, parity):
                t3, t2 = v + 1, v + 2
                if not active(t3) and not active(t2):
                    return
                wait(dve, s_xx, (t2 if active(t2) else t3) + 1)
                wait(dve, s_prod[1], v * PRODS[1])
                wait(dve, s_prod[0], (v + 1) * PRODS[0])
                k0, k1 = (0 if active(t3) else 1), (2 if active(t2) else 1)
                nc.vector.tensor_scalar(xc[:, 1 - parity, k0:k1, :], xx[:, bass.ds(t3 + k0, k1 - k0), :],
                                        wpow[:, 0:1], None, ALU.mult).then_inc(s_xc, 1)

            def fma(layer, t, q, parity):
                n, k = D_BANKS[layer][q // Q], q % Q
                j = n * Q + k
                if k == 0:
                    wait(dve, s_y[layer], t * BANKS + n + 1)
                dst = acc[layer][:, k * P:(k + 1) * P]
                if q < Q:
                    wait(dve, s_prod[layer], t * PRODS[layer] + k + 1)
                    if k == 0:
                        wait(dve, s_epi[layer + 1], (t - 1) * (EPI2, EPI3)[layer] + 1)
                    add = prods[:, 0, k * P:(k + 1) * P]
                else:
                    wait(dve, s_fma[layer], t * FMAS[layer] + q - Q + 1)
                    add = dst
                nc.vector.scalar_tensor_tensor(dst, ybank[n % RING][:, k * P:(k + 1) * P],
                                               xc[:, parity, 1 - layer, j:j + 1], add, ALU.mult,
                                               ALU.add).then_inc(s_fma[layer], 1)

            def scale(l, t, parity, i, s, done):
                wait(dve, s, done + i)
                if i == 0:
                    nc.vector.tensor_scalar(mx[l][:, 1:2], mx[l][:, 0:1], TINY, HALF_RANGE, ALU.max,
                                            ALU.mult).then_inc(s, 1)
                elif i == 1:
                    nc.vector.tensor_scalar(mp[l][:, parity:parity + 1].bitcast(u32), mx[l][:, 1:2].bitcast(u32),
                                            EXPONENT, None, ALU.bitwise_and).then_inc(s, 1)
                else:
                    wait(dve, s_hi[l], t)
                    nc.vector.reciprocal(sc[l][:], mp[l][:, parity:parity + 1]).then_inc(s, 1)

            def relu_max(l, t, s, done):
                wait(dve, s, done)
                wait(dve, s_pool[l], t + 1)
                wait(dve, s_hi[l], t)
                nc.vector.tensor_scalar(r[l][:], pre[l][:], 0.0, None, ALU.max, ALU.max,
                                        accum_out=mx[l][:, 0:1]).then_inc(s, 1)

            def lo_part(l, t):
                n = (EPI1, EPI2)[l]
                wait(dve, s_hi[l], t + 1)
                wait(dve, s_xt[l], t)
                wait(dve, s_epi[l], t * n + n - 1)
                nc.vector.scalar_tensor_tensor(lo[l][:], r[l][:], sc[l][:], hi[l][:], ALU.mult,
                                               ALU.subtract).then_inc(s_epi[l], 1)

            def merge(layer, t, parity, i, s, done):
                if i == 0:
                    wait(dve, s_fma[layer], (t + 1) * FMAS[layer])
                    nc.vector.tensor_tensor(hs[layer][:], acc[layer][:, 0:2 * P], acc[layer][:, 2 * P:4 * P],
                                            ALU.add).then_inc(s, 1)
                elif i == 1:
                    wait(dve, s_sum[layer], (t + 1) * SUMS[layer])
                    wait(dve, s, done + 1)
                    nc.vector.tensor_tensor(hs[layer][:], hs[layer][:], half[layer][:], ALU.add).then_inc(s, 1)
                elif i == 2:
                    wait(dve, s, done + 2)
                    nc.vector.tensor_tensor(ssum[layer][:], hs[layer][:, 0:P], hs[layer][:, P:2 * P],
                                            ALU.add).then_inc(s, 1)
                else:
                    wait(dve, s, done + 3)
                    nc.vector.scalar_tensor_tensor(pre[layer + 1][:], ssum[layer][:], mp[layer][:, parity:parity + 1],
                                                   bcin[:, layer + 1, :], ALU.mult, ALU.add).then_inc(s, 1)

            def epilogue1(t, parity, i):
                s, done = s_epi[0], t * EPI1
                if i == 0:
                    wait(dve, s_l1, t + 1)
                    wait(dve, s_epi0, t * EPI0 + 5)
                    nc.vector.scalar_tensor_tensor(pre[0][:], misc[0][:, 0:P], msq[:, parity:parity + 1],
                                                   bcin[:, 0, :], ALU.mult, ALU.add).then_inc(s, 1)
                elif i == 1:
                    relu_max(0, t, s, done + 1)
                else:
                    scale(0, t, parity, i - 2, s, done + 2)

            def epilogue2(t, parity, i):
                s, done = s_epi[1], t * EPI2
                if i < 4:
                    merge(0, t, parity, i, s, done)
                elif i == 4:
                    relu_max(1, t, s, done + 4)
                else:
                    scale(1, t, parity, i - 5, s, done + 5)

            def epilogue3(t, parity, i):
                s, done = s_epi[2], t * EPI3
                if i < 4:
                    merge(1, t, parity, i, s, done)
                else:
                    wait(dve, s, done + 4)
                    wait(dve, s_pool[2], t + 1)
                    nc.vector.tensor_scalar(r[2][:], pre[2][:], 0.0, None, ALU.max).then_inc(s, 1)

            def x0_over_e(b):
                nc.vector.tensor_reduce(low[:, b, 0:F], emb[:, b, :, :], axis=AX.X, op=ALU.add).then_inc(s_low, 1)

            def step(v, parity):
                t1, t2, t3 = v + 2, v + 1, v
                other = 1 - parity
                wait(dve, s_xc, v + 2)
                if isinstance(v, int) and v == TILES - 1:
                    x0_over_e(NB - 1)
                for n in range(2 * BANKS):
                    layer, m = n // BANKS, n % BANKS
                    if m not in D_BANKS[layer]:
                        continue
                    for k in range(Q):
                        if active((t2, t3)[layer]):
                            fma(layer, (t2, t3)[layer], D_BANKS[layer].index(m) * Q + k, parity)
                        slot = n * Q + k
                        if 24 <= slot < 28 and active(t1):
                            epilogue1(t1, parity, slot - 24)
                        if slot == 32 and active(t1):
                            epilogue1(t1, parity, 4)
                        if 33 <= slot < 36 and active(t3 - 1):
                            epilogue3(t3 - 1, other, slot - 33)
                        if 40 <= slot < 42 and active(t3 - 1):
                            epilogue3(t3 - 1, other, slot - 37)
                        if 42 <= slot < 44 and active(t1 + 2):
                            x0_scale(t1 + 2, parity, slot - 42)
                        if slot == 68 and active(t2):
                            epilogue2(t2, other, 0)
                        if 76 <= slot < 80 and active(t2):
                            epilogue2(t2, other, slot - 75)
                        if 84 <= slot < 87 and active(t2):
                            epilogue2(t2, other, slot - 79)
                    if n == 10:
                        if active(t1 + 2):
                            for i in (2, 3, 4):
                                x0_scale(t1 + 2, parity, i)
                        if active(t1):
                            lo_part(0, t1)
                    if n == 13:
                        columns(v, parity)
                        if isinstance(v, int) and TILES - NB <= v < TILES - 1:
                            x0_over_e(v - TILES + NB)
                    if n == 15 and active(t1 + 2):
                        x0_lo(t1 + 2)
                if active(t2):
                    lo_part(1, t2)
                if active(t1 + 1):
                    squares_lo(t1 + 1)
                    stacked_lo(t1 + 1)

            steps(dve, step)
            for i in range(EPI3):
                epilogue3(TILES - 1, 1, i)


def pair_rows():
    pairs = [(i, (i + d) % F) for d in range(SHIFTS) for i in range(F)][:PAIRS]
    first = np.array([i * F + j for i, j in pairs])
    second = np.array([j * F + i for i, j in pairs])
    return first, second


def kernel(**inputs):
    import concourse.bacc as bacc
    from concourse.bass_utils import run_bass_kernel_spmd

    nc = bacc.Bacc("TRN2", target_bir_lowering=False, num_devices=1)
    arrays = {}

    def given(name, a):
        a = np.ascontiguousarray(a)
        arrays[name] = a
        return nc.dram_tensor(name, a.shape, mybir.dt.from_np(a.dtype), kind="ExternalInput").ap()

    first, second = pair_rows()
    w1 = np.asarray(inputs["L0_rec_W1"])

    def copied(a):
        for c in COPIES[1:]:
            a[Z - P + c:Z - P + c + REST] = a[Z - P:Z - P + REST]
        return a

    def by_tile(a):
        return a.reshape(KT, P, -1).transpose(1, 0, 2)

    def weights(rows, off_diagonal):
        w = np.zeros((Z, P), w1.dtype)
        w[off_diagonal:PAIRS] = w1[rows[off_diagonal:]]
        return by_tile(copied(w))

    members = np.zeros((Z, F), np.float32)
    members[np.arange(PAIRS), first // F] = 1
    members[np.arange(PAIRS), first % F] = 1
    distinct = members.copy()
    distinct[:F] = 0
    select = copied(members).T.astype(np.float16)

    ids = given("ids", inputs["ids"])
    tables = [given(f"tbl_{f}", inputs[f"tbl_{f}"]) for f in range(F)]
    args = [
        given("dense_ctx", inputs["dense_ctx"]),
        given("select", np.concatenate([select, select])),
        given("pairs_of", by_tile(distinct)),
        given("w_pair", weights(first, 0)),
        given("w_pair_t", weights(second, F)),
        given("w2", np.asarray(inputs["L0_rec_W2"]).reshape(P, F * P)),
        given("w3", np.asarray(inputs["L0_rec_W3"]).reshape(P, F * P)),
        [given(f"b{l}", inputs[f"L0_rec_b{l}"]) for l in (1, 2, 3)],
        given("W_top1", inputs["W_top1"]), given("b_top1", inputs["b_top1"]),
        given("W_top2", inputs["W_top2"]), given("b_top2", inputs["b_top2"]),
        given("W_top3", inputs["W_top3"]),
    ]
    out = nc.dram_tensor("out", (B, 1), mybir.dt.float32, kind="ExternalOutput").ap()
    build(nc, ids, tables, *args, out)
    result = run_bass_kernel_spmd(nc, [arrays], core_ids=[0])
    return result.results[0]["out"]
```
